# Optimizing a Trainium2 kernel written in Bass

```python
import numpy as np
import jax
import jax.numpy as jnp

def _softmax(x, axis=-1):
    return jax.nn.softmax(x, axis=axis)

def _gelu(x):
    return jax.nn.gelu(x, approximate=True)

def _silu(x):
    return jax.nn.silu(x)

def _sigmoid(x):
    return jax.nn.sigmoid(x)

def _layernorm(x, axis=-1, eps=1e-05):
    m = jnp.mean(x, axis=axis, keepdims=True)
    v = jnp.var(x, axis=axis, keepdims=True)
    return (x - m) / jnp.sqrt(v + eps)

def _scatter_add(tgt, idx, src, axis=0):
    return tgt.at[idx].add(src)

def _segment_sum(src, seg, n):
    return jax.ops.segment_sum(src, seg, n)
kernel_name = 'mk_xattn_ffn_d1_seqx_r4_22bbc0'

def setup_inputs(seed: int=0):
    np.random.seed(seed)
    _w = jnp.asarray

    def _rec_inputs():
        import jax
        import jax.numpy as jnp
        _rk = jax.random.key(seed)
        x = 0.0003765 + 1 * jax.random.normal(jax.random.fold_in(_rk, 1), (8, 256, 512), jnp.float32)
        _lenS = 256 - jax.random.randint(jax.random.fold_in(_rk, 7), (8,), 0, max(1, 256 // 4) + 1, jnp.int32)
        _lenS2 = 256 - jax.random.randint(jax.random.fold_in(_rk, 8), (8,), 0, max(1, 256 // 4) + 1, jnp.int32)
        _ctx_2048P = jax.random.normal(jax.random.fold_in(_rk, 11), (8, 16, 512), jnp.float32)
        _ctx_2048c = jax.random.dirichlet(jax.random.fold_in(_rk, 511), 0.3 * jnp.ones((16,), jnp.float32), (8, 256))
        _ctx_2048t = jnp.einsum('bsk,bkd->bsd', _ctx_2048c, _ctx_2048P)
        _ctx_2048t = _ctx_2048t * jax.lax.rsqrt(jnp.mean(jnp.square(_ctx_2048t)) + 1e-12) * 0.953939
        ctx_2048 = -0.000292821 + 1.00034 * (_ctx_2048t + 0.3 * jax.random.normal(jax.random.fold_in(_rk, 611), (8, 256, 512), jnp.float32))
        return (x, ctx_2048)
    x, ctx_2048 = _rec_inputs()

    def _L0_xattn_setup():
        import jax, jax.numpy as jnp
        import numpy as np
        key = jax.random.key(seed)
        k1, k2, k3, k4, k5 = jax.random.split(key, 5)
        B, D_MODEL, L = (2, 256, 512)
        HEAD_DIM = 8
        H = D_MODEL // HEAD_DIM
        return {'k': jax.random.normal(k1, (B, D_MODEL, L), dtype=jnp.float32), 'v': jax.random.normal(k2, (B, D_MODEL, L), dtype=jnp.float32), 'q': jax.random.normal(k3, (B, D_MODEL, L), dtype=jnp.float32), 'ssm_kernel': jax.random.normal(k4, (H, L), dtype=jnp.float32), 'D': jax.random.normal(k5, (H,), dtype=jnp.float32), 'head_dim': HEAD_DIM}
    _L0_xattn_all = _L0_xattn_setup()
    _L0_xattn_in = {k: v for k, v in _L0_xattn_all.items() if k in ('ssm_kernel', 'D')}
    del _L0_xattn_all

    def _L0_ffn_setup():
        import jax, jax.numpy as jnp
        import numpy as np
        B, S, DIM = (2, 512, 512)
        E, K = (8, 2)
        H = DIM * 4 // 3
        key = jax.random.key(seed)
        ks = jax.random.split(key, 8)
        s = 0.02
        x = jax.random.normal(ks[0], (B, S, DIM), dtype=jnp.float32)
        sw1 = jax.random.normal(ks[1], (H, DIM), dtype=jnp.float32) * s
        sw2 = jax.random.normal(ks[2], (DIM, H), dtype=jnp.float32) * s
        sw3 = jax.random.normal(ks[3], (H, DIM), dtype=jnp.float32) * s
        ew1 = jax.random.normal(ks[4], (E, H, DIM), dtype=jnp.float32) * s
        ew2 = jax.random.normal(ks[5], (E, DIM, H), dtype=jnp.float32) * s
        ew3 = jax.random.normal(ks[6], (E, H, DIM), dtype=jnp.float32) * s
        wr = jax.random.normal(ks[7], (E, DIM), dtype=jnp.float32) * s
        return {'x': x, 'sw1': sw1, 'sw2': sw2, 'sw3': sw3, 'ew1': ew1, 'ew2': ew2, 'ew3': ew3, 'wr': wr}
    _L0_ffn_all = _L0_ffn_setup()
    _L0_ffn_in = {k: v for k, v in _L0_ffn_all.items() if k in ('sw1', 'sw2', 'sw3', 'ew1', 'ew2', 'ew3', 'wr')}
    del _L0_ffn_all
    return {'x': x, 'ctx_2048': ctx_2048, 'L0_xattn_ssm_kernel': _L0_xattn_in['ssm_kernel'], 'L0_xattn_D': _L0_xattn_in['D'], 'L0_ffn_sw1': _L0_ffn_in['sw1'], 'L0_ffn_sw2': _L0_ffn_in['sw2'], 'L0_ffn_sw3': _L0_ffn_in['sw3'], 'L0_ffn_ew1': _L0_ffn_in['ew1'], 'L0_ffn_ew2': _L0_ffn_in['ew2'], 'L0_ffn_ew3': _L0_ffn_in['ew3'], 'L0_ffn_wr': _L0_ffn_in['wr']}

def reference(x, ctx_2048, L0_xattn_ssm_kernel, L0_xattn_D, L0_ffn_sw1, L0_ffn_sw2, L0_ffn_sw3, L0_ffn_ew1, L0_ffn_ew2, L0_ffn_ew3, L0_ffn_wr):
    import jax
    import jax.numpy as jnp

    def _L0_xattn_ref(k, v, q, ssm_kernel, D, head_dim):
        import jax, jax.numpy as jnp
        import numpy as np
        B, HD, L = k.shape
        H = HD // head_dim
        fft_size = 2 * L
        k_ = k.reshape(B, H, head_dim, L)
        v_ = v.reshape(B, H, head_dim, L)
        q_ = q.reshape(B, H, head_dim, L)
        kv = jnp.einsum('bhil,bhjl->bijhl', k_, v_)
        kv_f = jnp.fft.rfft(kv, n=fft_size)
        kernel_f = jnp.fft.rfft(ssm_kernel, n=fft_size)
        y = jnp.fft.irfft(kv_f * kernel_f, n=fft_size)[..., :L]
        out = y + kv * D[None, None, None, :, None]
        out = jnp.einsum('bijhl,bhil->bjhl', out, q_)
        out = jnp.transpose(out, (0, 2, 1, 3)).reshape(B, H * head_dim, L)
        return out.astype(k.dtype)

    def _L0_ffn_ref(x, sw1, sw2, sw3, ew1, ew2, ew3, wr):
        import jax, jax.numpy as jnp
        import numpy as np
        B, S, DIM = (2, 512, 512)
        E, K = (8, 2)
        H = DIM * 4 // 3
        shared = jax.nn.silu(x @ sw1.T) * (x @ sw3.T) @ sw2.T
        logits = x @ wr.T
        probs = jax.nn.softmax(logits, axis=-1)
        top_p, top_i = jax.lax.top_k(probs, K)
        top_p = top_p / jnp.sum(top_p, axis=-1, keepdims=True)
        gates = jnp.sum(jax.nn.one_hot(top_i, E, dtype=x.dtype) * top_p[..., None], axis=-2)
        u = jnp.einsum('bsd,ehd->bseh', x, ew1)
        v = jnp.einsum('bsd,ehd->bseh', x, ew3)
        h = jax.nn.silu(u) * v
        eo = jnp.einsum('bseh,edh->bsed', h, ew2)
        return shared + jnp.einsum('bsed,bse->bsd', eo, gates)
    x = x + _L0_xattn_ref(ctx_2048, ctx_2048, _layernorm(x, axis=-1), L0_xattn_ssm_kernel, L0_xattn_D, 8)
    x = x + _L0_ffn_ref(_layernorm(x, axis=-1), L0_ffn_sw1, L0_ffn_sw2, L0_ffn_sw3, L0_ffn_ew1, L0_ffn_ew2, L0_ffn_ew3, L0_ffn_wr)
    return x

_drawn_inputs = setup_inputs


def setup_inputs(seed=0):
    import zlib

    import numpy as np

    out = dict(_drawn_inputs(seed))
    spreads = {}
    factors = {'L0_ffn_sw1': 8.0,
     'L0_ffn_sw2': 8.0,
     'L0_ffn_sw3': 8.0,
     'L0_ffn_ew1': 8.0,
     'L0_ffn_ew2': 8.0,
     'L0_ffn_ew3': 8.0,
     'L0_ffn_wr': 8.0}
    for name, (base, spread) in spreads.items():
        noise = np.random.default_rng([zlib.crc32(name.encode()), seed]).standard_normal(out[name].shape)
        drawn = base * np.exp(spread * noise) if base else spread * noise
        out[name] = jnp.asarray(drawn.astype(out[name].dtype))
    for name, factor in factors.items():
        out[name] = (out[name] * factor).astype(out[name].dtype)
    return out
```

```python
from contextlib import ExitStack

import concourse.bass as bass
from concourse import mybir

F32 = mybir.dt.float32
F32R = mybir.dt.float32r
ALU = mybir.AluOpType
ACT = mybir.ActivationFunctionType
AX = mybir.AxisListType

P = 128
BATCH, CH, L = 8, 256, 512
HD = 8
HEADS = CH // HD
LB = L // P
TOK = BATCH * CH
TILES = TOK // P
HT = BATCH * HD
PAIRS = HT * HD
EXPERTS = 8
GROUPS = EXPERTS + 1
HID = L * 4 // 3
NC = HID // P
REM = HID - NC * P
TRIO = GROUPS // 3
LEFT = TRIO * REM
TB = TOK // 512
JOBS = 3 * NC
UNITS = TB * NC
KROW = P + L
EPS = 1e-5


def positive(value):
    return not isinstance(value, int) or value > 0


def build(nc, x, ctx_in, ssm_kernel, d_skip, sw1, sw2, sw3, ew1, ew2, ew3, wr, out):
    kpad = nc.dram_tensor("kpad", (HEADS, KROW), F32, kind="Internal").ap()
    gates_dram = nc.dram_tensor("gates_by_expert", (GROUPS, TOK), F32, kind="Internal").ap()

    base = 16512
    place = {"at": base}

    def sb(name, shape, dt=F32, at=None):
        size = 4
        for n in shape[1:]:
            size *= n
        if at is None:
            at = place["at"]
            place["at"] = at + (size + 31) // 32 * 32
        return nc.alloc_sbuf_tensor_at(name, shape, dt, offset=at)

    acc = sb("acc", [P, TILES, L])
    x_hi = sb("x_hi", [P, LB, TOK], F32R)
    x_lo = sb("x_lo", [P, LB, TOK], F32R)
    stage = place["at"]
    w1_hi = sb("w1_hi", [P, NC, LB, P], F32R)
    w1_lo = sb("w1_lo", [P, NC, LB, P], F32R)
    w3_hi = sb("w3_hi", [P, NC, LB, P], F32R)
    w3_lo = sb("w3_lo", [P, NC, LB, P], F32R)
    w2_hi = sb("w2_hi", [P, NC, L], F32R)
    w2_lo = sb("w2_lo", [P, NC, L], F32R)
    h_hi = sb("h_hi", [P, NC, 512], F32R)
    h_lo = sb("h_lo", [P, NC, 512], F32R)
    silu_u = sb("silu_u", [P, 512])
    hidden = sb("hidden", [P, 512])
    router_area = place["at"]
    gate_rows = sb("gate_rows", [P, 2, TRIO, 512])
    stage_end = place["at"]
    w1_raw = sb("w1_raw", [P, 2, L])
    w3_raw = sb("w3_raw", [P, 2, L])
    w2_raw = sb("w2_raw", [P, 2, LB, P])
    ident = sb("ident", [P, P])
    minus_half = sb("minus_half", [P, 1])
    gates = sb("gates", [P, GROUPS, TILES])
    stats = sb("stats", [P, 2, 6])
    moments = sb("moments", [P, 2, 2])
    var_eps = sb("var_eps", [P, 2])
    minus_mean = sb("minus_mean", [P, 2])
    rstd = sb("rstd", [P, 2])
    shift = sb("shift", [P, 2])
    wr_hi = sb("wr_hi", [P, LB, EXPERTS], F32R)
    wr_lo = sb("wr_lo", [P, LB, EXPERTS], F32R)
    assert place["at"] <= 229368, place["at"]
    place["at"] = stage
    x_raw = sb("x_raw", [P, 2, L])
    c_raw = sb("c_raw", [P, 2, L])
    c_rev = sb("c_rev", [P, L])
    xn = sb("xn", [P, 2, L])
    yn = sb("yn", [P, L])
    qT = sb("qT", [P, 2, LB, P])
    cT = sb("cT", [P, 2, LB, P])
    t_raw = sb("t_raw", [P, 2, L])
    t_hi = sb("t_hi", [P, 2, L], F32R)
    t_lo = sb("t_lo", [P, 2, L], F32R)
    kv = sb("kv", [P, 2, PAIRS])
    kv_hi = sb("kv_hi", [P, 2, LB, PAIRS], F32R)
    kv_lo = sb("kv_lo", [P, 2, LB, PAIRS], F32R)
    scaled = sb("scaled", [P, 2, PAIRS])
    attnT = sb("attnT", [P, 2, LB, P])
    krows = sb("krows", [HEADS, KROW])
    d_col = sb("d_col", [HEADS, 1])
    assert place["at"] <= router_area, (place["at"], router_area)
    place["at"] = router_area
    logitsT = sb("logitsT", [EXPERTS, TB, 512])
    wr_rows = sb("wr_rows", [EXPERTS, L])
    assert place["at"] <= stage_end
    place["at"] = router_area
    larger = sb("larger", [P, TILES, EXPERTS, EXPERTS])
    equal = sb("equal", [P, TILES, EXPERTS, EXPERTS])
    before = sb("before", [P, EXPERTS, EXPERTS])
    logits = sb("logits", [P, TILES, EXPERTS])
    probs = sb("probs", [P, TILES, EXPERTS])
    rank = sb("rank", [P, TILES, EXPERTS])
    per_tile = sb("per_tile", [P, 4, TILES])
    gatesT = sb("gatesT", [P, 2, P])
    assert place["at"] <= stage_end

    with ExitStack() as stack:
        def sem(name):
            return stack.enter_context(nc.semaphore(name))

        banks = [stack.enter_context(nc.psum_tensor(f"bank{i}", [P, 512], F32)) for i in range(8)]
        conv_ps = banks[0:4]
        q_ps, c_ps, attn_ps, yn_ps = banks[4], banks[5], banks[6], banks[7]
        out_ps, u_ps, v_ps, w_ps = banks[0:4], banks[4], banks[5], banks[6:8]
        router_ps = banks[5]

        zeroed = sem("zeroed"); ident_ready = sem("ident_ready"); kern_in = sem("kern_in")
        kern_skip = sem("kern_skip"); kpad_written = sem("kpad_written")
        x_in = [sem(f"x_in{i}") for i in range(2)]
        c_in = [sem(f"c_in{i}") for i in range(2)]
        t_in = [sem(f"t_in{i}") for i in range(2)]
        ln_steps = sem("ln_steps"); rstd_ready = sem("rstd_ready"); shift_ready = sem("shift_ready")
        c_reversed = sem("c_reversed"); xn_ready = sem("xn_ready")
        q_turned = sem("q_turned"); c_turned = sem("c_turned")
        qT_ready = sem("qT_ready"); cT_ready = sem("cT_ready")
        t_hi_ready = sem("t_hi_ready"); t_lo_ready = sem("t_lo_ready")
        kv_ready = sem("kv_ready"); kv_hi_ready = sem("kv_hi_ready"); kv_lo_ready = sem("kv_lo_ready")
        conv_done = sem("conv_done"); scaled_ready = sem("scaled_ready"); attn_ready = sem("attn_ready")
        attn_turned = sem("attn_turned"); acc_written = sem("acc_written"); yn_ready = sem("yn_ready")
        yn_turned = sem("yn_turned"); x_hi_ready = sem("x_hi_ready"); x_lo_ready = sem("x_lo_ready")
        wr_in = sem("wr_in"); wr_turned = sem("wr_turned"); wr_hi_ready = sem("wr_hi_ready")
        wr_lo_ready = sem("wr_lo_ready"); logits_done = sem("logits_done")
        logitsT_ready = sem("logitsT_ready"); logits_turned = sem("logits_turned")
        before_ready = sem("before_ready"); route_steps = sem("route_steps"); exp_ready = sem("exp_ready")
        gates_ready = sem("gates_ready"); gates_turned = sem("gates_turned")
        gatesT_ready = sem("gatesT_ready"); gates_written = sem("gates_written")
        w_in = [sem(f"w_in{i}") for i in range(2)]
        w_turned = sem("w_turned"); w_hi_ready = sem("w_hi_ready"); w_lo_ready = sem("w_lo_ready")
        u_done = sem("u_done"); v_done = sem("v_done"); silu_ready = sem("silu_ready")
        hidden_ready = sem("hidden_ready"); gated_ready = sem("gated_ready")
        h_hi_ready = sem("h_hi_ready"); h_lo_ready = sem("h_lo_ready")
        out_done = sem("out_done")
        rows_in = [sem(f"rows_in{i}") for i in range(2)]
        out_written = sem("out_written")

        x_heads = x.rearrange("b (t s j) l -> t s b j l", s=2, j=HD)
        c_heads = ctx_in.rearrange("b (t s j) l -> t s b j l", s=2, j=HD)
        out_heads = out.rearrange("b (t s j) l -> t s b j l", s=2, j=HD)

        def split3(hi_a, lo_a, hi_b, lo_b):
            return ((hi_a, hi_b), (hi_a, lo_b), (lo_a, hi_b))

        block = stack.enter_context(nc.Block())

        @block.sync
        def _(sp):
            sp.dma_start(krows[:, P:KROW], ssm_kernel).then_inc(kern_in, 16)
            sp.dma_start(d_col[:, :], d_skip.rearrange("(h o) -> h o", o=1)).then_inc(kern_in, 16)

            def load_tile(t, p):
                if not (isinstance(t, int) and t < 2):
                    used = sp.to_reg(t - 1)
                    sp.wait_ge(xn_ready, used)
                    sp.wait_ge(c_reversed, used)
                for s in range(2):
                    sp.dma_start(acc[s * HT:(s + 1) * HT, bass.ds(t, 1), :].rearrange("p o l -> p (o l)"),
                                 x_heads[bass.ds(t, 1), s, :, :, :].rearrange("o b j l -> (o b) j l")
                                 ).then_inc(x_in[p], 16)
                    for raw, heads, landed in ((x_raw, x_heads, x_in), (c_raw, c_heads, c_in)):
                        sp.dma_start(raw[s * HT:(s + 1) * HT, p, :],
                                     heads[bass.ds(t, 1), s, :, :, :].rearrange("o b j l -> (o b) j l")
                                     ).then_inc(landed[p], 16)

            def load_table(t, s):
                if not (isinstance(t, int) and t < 1):
                    used = sp.to_reg(2 * t + s - 1)
                    sp.wait_ge(t_lo_ready, used)
                sp.dma_start(t_raw[:, s, :],
                             bass.AP(kpad.tensor, t * (2 * KROW) + (s * KROW + 1), [[1, P], [1, L]])
                             ).then_inc(t_in[s], 16)

            load_tile(0, 0)
            load_tile(1, 1)
            sp.wait_ge(kern_skip, 1)
            sp.wait_ge(zeroed, 2)
            sp.dma_start(kpad, krows[:, :]).then_inc(kpad_written, 16)
            sp.wait_ge(kpad_written, 16)
            load_table(0, 0)
            load_table(0, 1)
            load_table(1, 0)
            load_table(1, 1)
            with sp.Fori(1, TILES // 2) as half:
                for p in range(2):
                    load_tile(2 * half + p, p)
                    load_table(2 * half + p, 0)
                    load_table(2 * half + p, 1)

            def slot_free(e, c):
                return e * JOBS + (0 if c == 0 else -3 if c == 1 else 3 * c - 3)

            def load_chunk(e, c, w1, w3, w2):
                free = slot_free(e, c)
                if positive(free):
                    if not isinstance(free, int):
                        free = sp.to_reg(free)
                    sp.wait_ge(w_turned, free)
                for raw, w in ((w1_raw, w1), (w3_raw, w3)):
                    sp.dma_start(raw[:, c % 2, :], w[c * P:(c + 1) * P, :]).then_inc(w_in[c % 2], 16)
                sp.dma_start(w2_raw[:, c % 2, :, :],
                             w2[:, c * P:(c + 1) * P].rearrange("(d p) h -> p d h", p=P)
                             ).then_inc(w_in[c % 2], 16)

            for c in range(NC):
                load_chunk(0, c, sw1, sw3, sw2)
                if c == 1:
                    sp.dma_start(wr_rows[:, :], wr).then_inc(wr_in, 16)
            with sp.Fori(1, GROUPS) as e:
                for c in range(NC):
                    load_chunk(e, c, *(w[bass.ds(e - 1, 1), :, :].rearrange("o r c -> (o r) c")
                                       for w in (ew1, ew3, ew2)))

            sp.wait_ge(gatesT_ready, 2)
            gate_dst = gates_dram.rearrange("e (t p) -> (e t) p", p=P)
            sp.dma_start(gate_dst[0:P, :], gatesT[:, 0, :]).then_inc(gates_written, 16)
            sp.dma_start(gate_dst[P:GROUPS * TILES, :], gatesT[0:GROUPS * TILES - P, 1, :]).then_inc(gates_written, 16)
            sp.wait_ge(gates_written, 32)

            def load_rows(tb):
                for g in range(TRIO):
                    for i in range(TRIO):
                        e = TRIO * g + i
                        sp.dma_start(gate_rows[i * REM:(i + 1) * REM, tb % 2, g, :],
                                     bass.AP(gates_dram.tensor, e * TOK + tb * 512, [[0, REM], [1, 512]])
                                     ).then_inc(rows_in[tb % 2], 16)

            load_rows(0)
            load_rows(1)
            for g in range(TRIO):
                sp.wait_ge(w_turned, slot_free(GROUPS, g))
                for i in range(TRIO):
                    e = TRIO * g + i
                    w1, w3, w2 = (sw1, sw3, sw2) if e == 0 else (ew1[e - 1], ew3[e - 1], ew2[e - 1])
                    mine = slice(i * REM, (i + 1) * REM)
                    for raw, w in ((w1_raw, w1), (w3_raw, w3)):
                        sp.dma_start(raw[mine, g % 2, :], w[NC * P:HID, :]).then_inc(w_in[g % 2], 16)
                    sp.dma_start(w2_raw[:, g % 2, :, mine],
                                 w2[:, NC * P:HID].rearrange("(d p) h -> p d h", p=P)
                                 ).then_inc(w_in[g % 2], 16)
            for tb in range(2, TB):
                sp.wait_ge(gated_ready, TRIO * (tb - 1))
                load_rows(tb)

            added = TILES + GROUPS * TILES
            with sp.Fori(0, TILES) as t:
                tile_added = sp.to_reg(t + (added + 1))
                sp.wait_ge(acc_written, tile_added)
                for s in range(2):
                    sp.dma_start(out_heads[bass.ds(t, 1), s, :, :, :].rearrange("o b j l -> (o b) j l"),
                                 acc[s * HT:(s + 1) * HT, bass.ds(t, 1), :].rearrange("p o l -> p (o l)")
                                 ).then_inc(out_written, 16)
            sp.wait_ge(out_written, 16 * 2 * TILES)

        @block.gpsimd
        def _(pool):
            nc.gpsimd.memset(krows[:, 0:P], 0.0).then_inc(zeroed, 1)
            nc.gpsimd.memset(minus_half[:, :], -0.5).then_inc(zeroed, 1)
            nc.gpsimd.memset(ident[:, :], 0.0).then_inc(zeroed, 1)
            pool.wait_ge(zeroed, 3)
            nc.gpsimd.affine_select(out=ident[:, :], in_=ident[:, :], compare_op=ALU.not_equal, fill=1.0,
                                    base=0, pattern=[[-1, P]], channel_multiplier=1).then_inc(ident_ready, 1)

            def ln_tail(n, k):
                pool.wait_ge(ln_steps, 4 * n)
                nc.gpsimd.tensor_tensor(rstd[:, k:k + 1], var_eps[:, k:k + 1], minus_half[:, :], ALU.pow
                                        ).then_inc(rstd_ready, 1)
                pool.wait_ge(rstd_ready, n)
                nc.gpsimd.tensor_tensor(shift[:, k:k + 1], minus_mean[:, k:k + 1], rstd[:, k:k + 1], ALU.mult
                                        ).then_inc(shift_ready, 1)

            def split_table(g, s):
                pool.wait_ge(t_hi_ready, g + 1)
                if not (isinstance(g, int) and g < 2):
                    pool.wait_ge(conv_done, LB * (g - 1))
                nc.gpsimd.tensor_tensor(t_lo[:, s, :], t_raw[:, s, :], t_hi[:, s, :].bitcast(F32),
                                        ALU.subtract).then_inc(t_lo_ready, 1)

            def products(g, s, p):
                for k in range(LB):
                    n = g * LB + k
                    if k == 0:
                        pool.wait_ge(cT_ready, (g - s + 2) // 2 if isinstance(g, int) else tile_of[0] + 1)
                    if not (isinstance(n, int) and n < 2):
                        pool.wait_ge(kv_lo_ready, n - 1)
                    one = cT[:, p, k, s * HT:(s + 1) * HT].rearrange("p (b j) -> p b j", j=HD)
                    nc.gpsimd.tensor_tensor(kv[:, k % 2, :].rearrange("p (b j i) -> p b j i", j=HD, i=HD),
                                            one.unsqueeze(3).broadcast_to([P, BATCH, HD, HD]),
                                            one.unsqueeze(2).broadcast_to([P, BATCH, HD, HD]),
                                            ALU.mult).then_inc(kv_ready, 1)

            tile_of = [None]
            ln_tail(1, 0)
            split_table(0, 0)
            products(0, 0, 0)

            def step(s, p):
                last = isinstance(s, int) and s == TILES - 1
                first = isinstance(s, int) and s == 0
                if not last:
                    ln_tail(2 if first else 2 * s + 1, 0)
                split_table(2 * s + 1, 1)
                tile_of[0] = s
                products(2 * s + 1, 1, p)
                if not first:
                    ln_tail(2 * s + 1 if last else 2 * s + 2, 1)
                if not last:
                    split_table(2 * s + 2, 0)
                    tile_of[0] = s + 1
                    products(2 * s + 2, 0, 1 - p)

            step(0, 0)
            step(1, 1)
            with pool.Fori(1, TILES // 2 - 1) as half:
                step(2 * half, 0)
                step(2 * half + 1, 1)
            step(TILES - 2, 0)
            step(TILES - 1, 1)
            ln_tail(2 * TILES, 1)

            pool.wait_ge(logits_turned, 1)
            nc.gpsimd.memset(before[:, :, :], 1.0).then_inc(zeroed, 1)
            pool.wait_ge(zeroed, 4)
            nc.gpsimd.affine_select(out=before[:, :, :], in_=before[:, :, :], compare_op=ALU.is_gt, fill=0.0,
                                    base=0, pattern=[[1, EXPERTS], [-1, EXPERTS]], channel_multiplier=0
                                    ).then_inc(before_ready, 1)

        @block.scalar
        def _(act):
            def reverse_ctx(t, p, use):
                act.wait_ge(c_in[p], use)
                if not (isinstance(t, int) and t < 1):
                    act.wait_ge(c_turned, t)
                nc.scalar.activation(c_rev[:, :], c_raw[:, p, ::-1], ACT.Copy).then_inc(c_reversed, 1)

            def normalise_x(t, p, n):
                act.wait_ge(shift_ready, n)
                if not (isinstance(t, int) and t < 2):
                    act.wait_ge(q_turned, t - 1)
                nc.scalar.activation(xn[:, p, :], x_raw[:, p, :], ACT.Identity, bias=shift[:, 0:1],
                                     scale=rstd[:, 0:1]).then_inc(xn_ready, 1)

            def round_table(g, s, use):
                act.wait_ge(t_in[s], use)
                if not (isinstance(g, int) and g < 2):
                    act.wait_ge(conv_done, LB * (g - 1))
                nc.scalar.activation(t_hi[:, s, :], t_raw[:, s, :], ACT.Copy).then_inc(t_hi_ready, 1)

            def round_products(g, s):
                for k in range(LB):
                    act.wait_ge(kv_ready, g * LB + (k + 1))
                    if k == 0 and not (isinstance(g, int) and g < 2):
                        act.wait_ge(conv_done, LB * (g - 1))
                    nc.scalar.activation(kv_hi[:, s, k, :], kv[:, k % 2, :], ACT.Copy).then_inc(kv_hi_ready, 1)

            def keep_turned(t, p):
                act.wait_ge(q_turned, t + 1)
                if not (isinstance(t, int) and t < 2):
                    act.wait_ge(scaled_ready, 2 * LB * (t - 1))
                    act.wait_ge(kv_ready, 2 * LB * (t - 1))
                nc.scalar.activation(qT[:, p, :, :].rearrange("p k c -> p (k c)"), q_ps[:, :], ACT.Copy
                                     ).then_inc(qT_ready, 1)
                act.wait_ge(c_turned, t + 1)
                nc.scalar.activation(cT[:, p, :, :].rearrange("p k c -> p (k c)"), c_ps[:, :], ACT.Copy
                                     ).then_inc(cT_ready, 1)

            def normalise_y(t, n):
                act.wait_ge(shift_ready, n)
                if not (isinstance(t, int) and t < 1):
                    act.wait_ge(yn_turned, t)
                nc.scalar.activation(yn[:, :].unsqueeze(1), acc[:, bass.ds(t, 1), :], ACT.Identity,
                                     bias=shift[:, 1:2], scale=rstd[:, 1:2]).then_inc(yn_ready, 1)

            def round_x(t):
                act.wait_ge(yn_turned, t + 1)
                nc.scalar.activation(x_hi[:, :, bass.ds(t * P, P)], yn_ps[:, :].rearrange("p (k c) -> p k c", c=P),
                                     ACT.Copy).then_inc(x_hi_ready, 1)

            reverse_ctx(0, 0, 32)
            normalise_x(0, 0, 1)
            round_table(0, 0, 16)
            keep_turned(0, 0)
            round_products(0, 0)

            def step(s, p, nth):
                last = isinstance(s, int) and s == TILES - 1
                first = isinstance(s, int) and s == 0
                if not last:
                    fills = 32 * (nth + p) + 32
                    reverse_ctx(s + 1, 1 - p, fills)
                    normalise_x(s + 1, 1 - p, 2 if first else 2 * s + 1)
                if not (isinstance(s, int) and s < 2):
                    round_x(s - 2)
                round_table(2 * s + 1, 1, 16 * s + 16)
                round_products(2 * s + 1, 1)
                if not last:
                    keep_turned(s + 1, 1 - p)
                    round_table(2 * s + 2, 0, 16 * s + 32)
                if not first:
                    normalise_y(s - 1, 2 * s + 1 if last else 2 * s + 2)
                if not last:
                    round_products(2 * s + 2, 0)

            step(0, 0, 0)
            step(1, 1, 0)
            with act.Fori(1, TILES // 2 - 1) as half:
                step(2 * half, 0, half)
                step(2 * half + 1, 1, half)
            step(TILES - 2, 0, TILES // 2 - 1)
            step(TILES - 1, 1, TILES // 2 - 1)
            round_x(TILES - 2)
            normalise_y(TILES - 1, 2 * TILES)
            round_x(TILES - 1)

            def round_weights(e, c, m, rows):
                q = 3 * c + m
                job = e * JOBS + q
                act.wait_ge(w_turned, job + 1)
                if m == 0:
                    pass
                bank = w_ps[q % 2]
                if m < 2:
                    dst = (w1_hi, w3_hi)[m][:, c, :, 0:rows]
                    src = bank[:, :].rearrange("p (k c) -> p k c", c=P)[:, :, 0:rows]
                else:
                    dst, src = w2_hi[0:rows, c, :], bank[0:rows, :]
                nc.scalar.activation(dst, src, ACT.Copy).then_inc(w_hi_ready, 1)

            for c in range(NC):
                for m in range(3):
                    round_weights(0, c, m, P)

            act.wait_ge(wr_turned, 1)
            nc.scalar.activation(wr_hi[:, :, :], router_ps[:, 0:LB * EXPERTS].rearrange("p (k e) -> p k e", e=EXPERTS),
                                 ACT.Copy).then_inc(wr_hi_ready, 1)
            for tb in range(TB):
                act.wait_ge(logits_done, tb + 1)
                nc.scalar.activation(logitsT[:, tb, :], banks[tb][0:EXPERTS, :], ACT.Copy).then_inc(logitsT_ready, 1)
            act.wait_ge(route_steps, 3)
            nc.scalar.activation(probs[:, :, :], logits[:, :, :], ACT.Exp).then_inc(exp_ready, 1)

            def unit(n, c, rows, prep):
                act.wait_ge(u_done, n + 1)
                if positive(n):
                    act.wait_ge(hidden_ready, n)
                nc.scalar.activation(silu_u[0:rows, :], u_ps[0:rows, :], ACT.Silu).then_inc(silu_ready, 1)
                if prep:
                    round_weights(prep[0], prep[1], 0, prep[2])
                    round_weights(prep[0], prep[1], 1, prep[2])
                if rows == P:
                    act.wait_ge(hidden_ready, n + 1)
                else:
                    act.wait_ge(gated_ready, n - (GROUPS * UNITS - 1))
                nc.scalar.activation(h_hi[0:rows, c, :], hidden[0:rows, :], ACT.Copy).then_inc(h_hi_ready, 1)
                if prep:
                    round_weights(prep[0], prep[1], 2, prep[2])

            unit(0, 0, P, None)

            def token_block(first_unit, prep_group, next_rows=P):
                for c in range(1, NC + 1):
                    prep = None
                    if prep_group is not None:
                        group, chunks, rows = prep_group
                        if c - 1 < chunks:
                            prep = (group, c - 1, rows)
                    unit(first_unit + c, c % NC, P if c < NC else next_rows, prep)

            def expert(e, last):
                with act.Fori(0, TB - 1) as tb:
                    token_block(e * UNITS + tb * NC, None)
                if last:
                    token_block(e * UNITS + (TB - 1) * NC, (e + 1, TRIO, LEFT), LEFT)
                else:
                    token_block(e * UNITS + (TB - 1) * NC, (e + 1, NC, P))

            with act.Fori(0, GROUPS - 1) as e:
                expert(e, False)
            expert(GROUPS - 1, True)
            for n in range(1, TB * TRIO):
                unit(GROUPS * UNITS + n, n % TRIO, LEFT, None)

        @block.vector
        def _(dve):
            dve.wait_ge(kern_in, 32)
            nc.vector.tensor_tensor(krows[:, P:P + 1], krows[:, P:P + 1], d_col[:, :], ALU.add).then_inc(kern_skip, 1)

            def moments_of(src, n, k):
                stats_done = 4 * n - 3 if isinstance(n, int) else dve.to_reg(4 * n - 3)
                nc.vector.bn_stats(stats[:, k, :], src).then_inc(ln_steps, 1)
                dve.wait_ge(kern_in, 32)
                dve.wait_ge(ln_steps, stats_done)
                nc.vector.bn_aggr(moments[:, k, :], stats[:, k, :]).then_inc(ln_steps, 1)
                dve.wait_ge(ln_steps, 4 * n - 2)
                nc.vector.tensor_scalar(var_eps[:, k:k + 1], moments[:, k, 1:2], EPS, None, ALU.add
                                        ).then_inc(ln_steps, 1)
                nc.vector.tensor_scalar(minus_mean[:, k:k + 1], moments[:, k, 0:1], -1.0, None, ALU.mult
                                        ).then_inc(ln_steps, 1)

            def moments_x(t, p, n, use):
                if not isinstance(t, int):
                    t, use = dve.to_reg(t), dve.to_reg(use)
                dve.wait_ge(kern_in, 32)
                dve.wait_ge(x_in[p], use)
                if not (isinstance(t, int) and t < 1):
                    dve.wait_ge(xn_ready, t)
                moments_of(x_raw[:, p, :], n, 0)

            def split_block(g, s, k):
                dve.wait_ge(kv_hi_ready, g * LB + (k + 1))
                nc.vector.tensor_tensor(kv_lo[:, s, k, :], kv[:, k % 2, :], kv_hi[:, s, k, :].bitcast(F32),
                                        ALU.subtract).then_inc(kv_lo_ready, 1)

            def contract(g, s, p, k, tile):
                n = g * LB + (k + 1)
                dve.wait_ge(conv_done, n)
                if k == 0 and s == 0:
                    dve.wait_ge(qT_ready, tile + 1)
                q = qT[:, p, k, s * HT:(s + 1) * HT].rearrange("p (b i) -> p b i", i=HD)
                nc.vector.tensor_tensor(scaled[:, k % 2, :].rearrange("p (b j i) -> p b j i", j=HD, i=HD),
                                        conv_ps[k][:, :].rearrange("p (b j i) -> p b j i", j=HD, i=HD),
                                        q.unsqueeze(2).broadcast_to([P, BATCH, HD, HD]), ALU.mult
                                        ).then_inc(scaled_ready, 1)
                if k == 0 and s == 0 and not (isinstance(tile, int) and tile < 2):
                    dve.wait_ge(attn_turned, tile - 1)
                dve.wait_ge(scaled_ready, n)
                nc.vector.tensor_reduce(attnT[:, p, k, s * HT:(s + 1) * HT],
                                        scaled[:, k % 2, :].rearrange("p (n i) -> p n i", i=HD), AX.X, ALU.add
                                        ).then_inc(attn_ready, 1)

            def add_residual(t, p, n):
                dve.wait_ge(attn_turned, t + 1)
                nc.vector.tensor_tensor(acc[:, bass.ds(t, 1), :], attn_ps[:, :].unsqueeze(1),
                                        acc[:, bass.ds(t, 1), :], ALU.add).then_inc(acc_written, 1)
                dve.wait_ge(kern_in, 32)
                dve.wait_ge(acc_written, t + 1)
                if not (isinstance(t, int) and t < 1):
                    dve.wait_ge(yn_ready, t)
                moments_of(acc[:, bass.ds(t, 1), :], n, 1)

            def split_x(t):
                dve.wait_ge(x_hi_ready, t + 1)
                nc.vector.tensor_tensor(x_lo[:, :, bass.ds(t * P, P)], yn_ps[:, :].rearrange("p (k c) -> p k c", c=P),
                                        x_hi[:, :, bass.ds(t * P, P)].bitcast(F32), ALU.subtract
                                        ).then_inc(x_lo_ready, 1)

            moments_x(0, 0, 1, 64)
            for k in range(LB):
                split_block(0, 0, k)

            def step(s, p, nth):
                last = isinstance(s, int) and s == TILES - 1
                first = isinstance(s, int) and s == 0
                if not last:
                    moments_x(s + 1, 1 - p, 2 if first else 2 * s + 1, 64 * (nth + p) + 64)
                for k in range(LB):
                    split_block(2 * s + 1, 1, k)
                    contract(2 * s, 0, p, k, s)
                if not (isinstance(s, int) and s < 2):
                    split_x(s - 2)
                if not first:
                    add_residual(s - 1, 1 - p, 2 * s + 1 if last else 2 * s + 2)
                for k in range(LB):
                    if not last:
                        split_block(2 * s + 2, 0, k)
                    contract(2 * s + 1, 1, p, k, s)

            step(0, 0, 0)
            step(1, 1, 0)
            with dve.Fori(1, TILES // 2 - 1) as half:
                step(2 * half, 0, half)
                step(2 * half + 1, 1, half)
            step(TILES - 2, 0, TILES // 2 - 1)
            step(TILES - 1, 1, TILES // 2 - 1)
            split_x(TILES - 2)
            add_residual(TILES - 1, 1, 2 * TILES)
            split_x(TILES - 1)

            def split_weights(e, c, m, rows):
                q = 3 * c + m
                dve.wait_ge(w_hi_ready, e * JOBS + (q + 1))
                bank = w_ps[q % 2]
                if m < 2:
                    dst = (w1_lo, w3_lo)[m][:, c, :, 0:rows]
                    hi = (w1_hi, w3_hi)[m][:, c, :, 0:rows]
                    src = bank[:, :].rearrange("p (k c) -> p k c", c=P)[:, :, 0:rows]
                else:
                    dst, hi, src = w2_lo[0:rows, c, :], w2_hi[0:rows, c, :], bank[0:rows, :]
                nc.vector.tensor_tensor(dst, src, hi.bitcast(F32), ALU.subtract).then_inc(w_lo_ready, 1)

            for c in range(NC):
                for m in range(3):
                    split_weights(0, c, m, P)

            dve.wait_ge(wr_hi_ready, 1)
            nc.vector.tensor_tensor(wr_lo[:, :, :], router_ps[:, 0:LB * EXPERTS].rearrange("p (k e) -> p k e", e=EXPERTS),
                                    wr_hi[:, :, :].bitcast(F32), ALU.subtract).then_inc(wr_lo_ready, 1)
            nc.vector.memset(gates[:, 0, :], 1.0).then_inc(gates_ready, 1)
            by_tile = [P, TILES, EXPERTS]
            pairwise = [P, TILES, EXPERTS, EXPERTS]
            top, total, inverse, norm = (per_tile[:, i, :] for i in range(4))
            dve.wait_ge(logits_turned, 1)
            nc.vector.tensor_copy(logits[:, :, :], router_ps[:, 128:256].rearrange("p (t e) -> p t e", e=EXPERTS)
                                  ).then_inc(route_steps, 1)
            dve.wait_ge(route_steps, 1)
            nc.vector.tensor_reduce(top, logits[:, :, :], AX.X, ALU.max).then_inc(route_steps, 1)
            dve.wait_ge(route_steps, 2)
            nc.vector.tensor_tensor(logits[:, :, :], logits[:, :, :], top.unsqueeze(2).broadcast_to(by_tile),
                                    ALU.subtract).then_inc(route_steps, 1)
            dve.wait_ge(exp_ready, 1)
            nc.vector.tensor_reduce(total, probs[:, :, :], AX.X, ALU.add).then_inc(route_steps, 1)
            dve.wait_ge(route_steps, 4)
            nc.vector.reciprocal(inverse, total).then_inc(route_steps, 1)
            dve.wait_ge(route_steps, 5)
            nc.vector.tensor_tensor(probs[:, :, :], probs[:, :, :], inverse.unsqueeze(2).broadcast_to(by_tile),
                                    ALU.mult).then_inc(route_steps, 1)
            dve.wait_ge(route_steps, 6)
            other = probs[:, :, :].unsqueeze(2).broadcast_to(pairwise)
            mine = probs[:, :, :].unsqueeze(3).broadcast_to(pairwise)
            nc.vector.tensor_tensor(larger[:, :, :, :], other, mine, ALU.is_gt).then_inc(route_steps, 1)
            nc.vector.tensor_tensor(equal[:, :, :, :], other, mine, ALU.is_equal).then_inc(route_steps, 1)
            dve.wait_ge(route_steps, 8)
            dve.wait_ge(before_ready, 1)
            nc.vector.tensor_tensor(equal[:, :, :, :], equal[:, :, :, :],
                                    before[:, :, :].unsqueeze(1).broadcast_to(pairwise), ALU.mult
                                    ).then_inc(route_steps, 1)
            dve.wait_ge(route_steps, 9)
            nc.vector.tensor_tensor(larger[:, :, :, :], larger[:, :, :, :], equal[:, :, :, :], ALU.add
                                    ).then_inc(route_steps, 1)
            dve.wait_ge(route_steps, 10)
            nc.vector.tensor_reduce(rank[:, :, :], larger[:, :, :, :], AX.X, ALU.add).then_inc(route_steps, 1)
            dve.wait_ge(route_steps, 11)
            nc.vector.tensor_scalar(rank[:, :, :], rank[:, :, :], 1.5, None, ALU.is_lt).then_inc(route_steps, 1)
            dve.wait_ge(route_steps, 12)
            nc.vector.tensor_tensor(probs[:, :, :], probs[:, :, :], rank[:, :, :], ALU.mult).then_inc(route_steps, 1)
            dve.wait_ge(route_steps, 13)
            nc.vector.tensor_reduce(total, probs[:, :, :], AX.X, ALU.add).then_inc(route_steps, 1)
            dve.wait_ge(route_steps, 14)
            nc.vector.reciprocal(norm, total).then_inc(route_steps, 1)
            dve.wait_ge(route_steps, 15)
            nc.vector.tensor_tensor(gates[:, 1:GROUPS, :].rearrange("p e t -> p t e"), probs[:, :, :],
                                    norm.unsqueeze(2).broadcast_to(by_tile), ALU.mult).then_inc(gates_ready, 1)
            rest = GROUPS * TILES - P
            dve.wait_ge(gates_turned, 1)
            nc.vector.tensor_copy(gatesT[:, 0, :], router_ps[:, 256:256 + P]).then_inc(gatesT_ready, 1)
            nc.vector.tensor_copy(gatesT[0:rest, 1, :], router_ps[0:rest, 384:384 + P]).then_inc(gatesT_ready, 1)

            def add_out(blocks, e, tb, left):
                for i in range(4):
                    dve.wait_ge(out_done, 4 * blocks + (i + 1))
                    dve.wait_ge(acc_written, 4 * blocks + (i + 1))
                    tile = tb * 4 + i
                    scalar = 1.0 if left else gates[:, bass.ds(e, 1), bass.ds(tile, 1)].rearrange("p a b -> p (a b)")
                    nc.vector.scalar_tensor_tensor(out=acc[:, bass.ds(tile, 1), :].rearrange("p o l -> p (o l)"),
                                                   in0=out_ps[i][:, :], scalar=scalar,
                                                   in1=acc[:, bass.ds(tile, 1), :].rearrange("p o l -> p (o l)"),
                                                   op0=ALU.mult, op1=ALU.add).then_inc(acc_written, 1)

            def unit(n, c, rows, prep, adds=None):
                if prep:
                    split_weights(prep[0], prep[1], 0, prep[2])
                dve.wait_ge(silu_ready, n + 1)
                dve.wait_ge(v_done, n + 1)
                if positive(n):
                    dve.wait_ge(h_lo_ready, n)
                nc.vector.tensor_tensor(hidden[0:rows, :], silu_u[0:rows, :], v_ps[0:rows, :], ALU.mult
                                        ).then_inc(hidden_ready, 1)
                if rows == LEFT:
                    left = n - GROUPS * UNITS
                    tb = left // TRIO
                    if left % TRIO == 0:
                        dve.wait_ge(rows_in[tb % 2], 16 * GROUPS * (tb // 2 + 1))
                    dve.wait_ge(hidden_ready, n + 1)
                    nc.vector.tensor_tensor(hidden[0:rows, :], hidden[0:rows, :],
                                            gate_rows[0:rows, tb % 2, left % TRIO, :], ALU.mult
                                            ).then_inc(gated_ready, 1)
                if prep:
                    split_weights(prep[0], prep[1], 1, prep[2])
                dve.wait_ge(h_hi_ready, n + 1)
                nc.vector.tensor_tensor(h_lo[0:rows, c, :], hidden[0:rows, :], h_hi[0:rows, c, :].bitcast(F32),
                                        ALU.subtract).then_inc(h_lo_ready, 1)
                if prep:
                    split_weights(prep[0], prep[1], 2, prep[2])

            unit(0, 0, P, None)

            def token_block(e, tb, left_next, prep_group):
                first_unit = e * UNITS + tb * NC
                for c in range(1, NC + 1):
                    prep = None
                    if prep_group is not None and c - 1 < prep_group[1]:
                        prep = (prep_group[0], c - 1, prep_group[2])
                    unit(first_unit + c, c % NC, LEFT if left_next and c == NC else P, prep)
                add_out(e * TB + tb, e, tb, False)

            def expert(e, last):
                with dve.Fori(0, TB - 1) as tb:
                    token_block(e, tb, False, None)
                token_block(e, TB - 1, last, (e + 1, TRIO, LEFT) if last else (e + 1, NC, P))

            dve.wait_ge(gates_ready, 2)
            dve.wait_ge(x_lo_ready, TILES)
            with dve.Fori(0, GROUPS - 1) as e:
                expert(e, False)
            expert(GROUPS - 1, True)
            for n in range(1, TB * TRIO):
                unit(GROUPS * UNITS + n, n % TRIO, LEFT, None)
                if n % TRIO == 0:
                    add_out(GROUPS * TB + n // TRIO - 1, 0, n // TRIO - 1, True)
            add_out(GROUPS * TB + TB - 1, 0, TB - 1, True)

        @block.tensor
        def _(pe):
            pe.wait_ge(ident_ready, 1)

            def turn(dst, src, rows=P, cols=P, step=P, signal=None, count=LB):
                for k in range(count):
                    last = nc.tensor.transpose(dst[0:cols, k * step:k * step + rows], src(k), ident[0:rows, 0:rows])
                last.then_inc(signal, 1)

            def turn_x_ctx(t, p):
                pe.wait_ge(xn_ready, t + 1)
                if not (isinstance(t, int) and t < 1):
                    pe.wait_ge(qT_ready, t)
                turn(q_ps, lambda k: xn[:, p, k * P:(k + 1) * P], signal=q_turned)
                pe.wait_ge(c_reversed, t + 1)
                if not (isinstance(t, int) and t < 1):
                    pe.wait_ge(cT_ready, t)
                turn(c_ps, lambda k: c_rev[:, (LB - 1 - k) * P:(LB - k) * P], signal=c_turned)

            def convolve(g, s):
                pe.wait_ge(t_lo_ready, g + 1)
                for lb in range(LB):
                    pe.wait_ge(kv_lo_ready, g * LB + (lb + 1))
                    if not (isinstance(g, int) and g < 1):
                        pe.wait_ge(scaled_ready, (g - 1) * LB + (lb + 1))
                    for mb in range(lb + 1):
                        d = lb - mb
                        passes = split3(t_hi[:, s, d * P:(d + 1) * P], t_lo[:, s, d * P:(d + 1) * P],
                                        kv_hi[:, s, mb, :], kv_lo[:, s, mb, :])
                        for i, (stationary, moving) in enumerate(passes):
                            last = nc.tensor.matmul(conv_ps[lb][:, :], stationary, moving,
                                                    start=(mb == 0 and i == 0), stop=(mb == lb and i == 2))
                    last.then_inc(conv_done, 1)

            def turn_attn(t, p):
                pe.wait_ge(attn_ready, 2 * LB * t + 2 * LB)
                if not (isinstance(t, int) and t < 1):
                    pe.wait_ge(acc_written, t)
                turn(attn_ps, lambda k: attnT[:, p, k, :], signal=attn_turned)

            def turn_y(t):
                pe.wait_ge(yn_ready, t + 1)
                if not (isinstance(t, int) and t < 1):
                    pe.wait_ge(x_lo_ready, t)
                turn(yn_ps, lambda k: yn[:, k * P:(k + 1) * P], signal=yn_turned)

            turn_x_ctx(0, 0)

            def step(s, p):
                last = isinstance(s, int) and s == TILES - 1
                first = isinstance(s, int) and s == 0
                convolve(2 * s, 0)
                if not last:
                    turn_x_ctx(s + 1, 1 - p)
                if not first:
                    turn_attn(s - 1, 1 - p)
                convolve(2 * s + 1, 1)
                if not first:
                    turn_y(s - 1)

            step(0, 0)
            step(1, 1)
            with pe.Fori(1, TILES // 2 - 1) as half:
                step(2 * half, 0)
                step(2 * half + 1, 1)
            step(TILES - 2, 0)
            step(TILES - 1, 1)
            turn_attn(TILES - 1, 1)
            turn_y(TILES - 1)

            def turn_weights(e, c, m, rows):
                q = 3 * c + m
                job = e * JOBS + q
                if m == 0:
                    if rows == P:
                        landed = 48 * (e * (3, 2)[c % 2] + (c // 2 + 1))
                    else:
                        landed = 48 * GROUPS * (3, 2)[c % 2] + 48 * TRIO * (c // 2 + 1)
                    pe.wait_ge(w_in[c % 2], landed)
                if q == 0:
                    if positive(job):
                        pe.wait_ge(w_lo_ready, job)
                elif positive(job - 1):
                    pe.wait_ge(w_lo_ready, job - 1)
                bank = w_ps[q % 2]
                if m < 2:
                    raw = (w1_raw, w3_raw)[m]
                    turn(bank, lambda k: raw[0:rows, c % 2, k * P:(k + 1) * P], rows=rows, signal=w_turned)
                else:
                    turn(bank, lambda k: w2_raw[:, c % 2, k, 0:rows], cols=rows, signal=w_turned)

            pe.wait_ge(x_lo_ready, TILES)
            for c in range(NC):
                for m in range(3):
                    turn_weights(0, c, m, P)

            pe.wait_ge(wr_in, 16)
            turn(router_ps, lambda k: wr_rows[:, k * P:(k + 1) * P], rows=EXPERTS, step=EXPERTS, signal=wr_turned)
            pe.wait_ge(wr_lo_ready, 1)
            for tb in range(TB):
                for k in range(LB):
                    cols = slice(tb * 512, (tb + 1) * 512)
                    passes = split3(wr_hi[:, k, :], wr_lo[:, k, :], x_hi[:, k, cols], x_lo[:, k, cols])
                    for i, (stationary, moving) in enumerate(passes):
                        last = nc.tensor.matmul(banks[tb][0:EXPERTS, :], stationary, moving,
                                                start=(k == 0 and i == 0), stop=(k == LB - 1 and i == 2))
                last.then_inc(logits_done, 1)
            for t in range(TILES):
                if t % 4 == 0:
                    pe.wait_ge(logitsT_ready, t // 4 + 1)
                last = nc.tensor.transpose(router_ps[:, 128 + t * EXPERTS:128 + (t + 1) * EXPERTS],
                                           logitsT[:, t // 4, (t % 4) * P:(t % 4 + 1) * P],
                                           ident[0:EXPERTS, 0:EXPERTS])
            last.then_inc(logits_turned, 1)
            pe.wait_ge(gates_ready, 2)
            nc.tensor.transpose(router_ps[:, 256:256 + P], gates[:, 0:EXPERTS, :].rearrange("p e t -> p (e t)"), ident[:, :])
            nc.tensor.transpose(router_ps[0:TILES, 384:384 + P], gates[:, EXPERTS, :], ident[:, :]
                                ).then_inc(gates_turned, 1)

            def up(n, e, tb, c, rows, which):
                bank = (u_ps, v_ps)[which]
                pe.wait_ge(w_lo_ready, e * JOBS + (3 * c + which + 1))
                if positive(n):
                    pe.wait_ge((silu_ready, hidden_ready)[which], n)
                w_hi, w_lo = ((w1_hi, w1_lo), (w3_hi, w3_lo))[which]
                for k in range(LB):
                    passes = split3(w_hi[:, c, k, 0:rows], w_lo[:, c, k, 0:rows],
                                    x_hi[:, k, bass.ds(tb * 512, 512)], x_lo[:, k, bass.ds(tb * 512, 512)])
                    for i, (stationary, moving) in enumerate(passes):
                        last = nc.tensor.matmul(bank[0:rows, :], stationary, moving,
                                                start=(k == 0 and i == 0), stop=(k == LB - 1 and i == 2))
                last.then_inc((u_done, v_done)[which], 1)

            def down(n, e, blocks, c, rows, chunks):
                pe.wait_ge(h_lo_ready, n + 1)
                pe.wait_ge(w_lo_ready, e * JOBS + (3 * c + 3))
                for i in range(4):
                    if c == 0:
                        pe.wait_ge(acc_written, TILES + 4 * blocks + (i - 3))
                    mine = slice(i * P, (i + 1) * P)
                    passes = split3(h_hi[0:rows, c, mine], h_lo[0:rows, c, mine], w2_hi[0:rows, c, :], w2_lo[0:rows, c, :])
                    for j, (stationary, moving) in enumerate(passes):
                        last = nc.tensor.matmul(out_ps[i][:, :], stationary, moving,
                                                start=(c == 0 and j == 0), stop=(c == chunks - 1 and j == 2))
                    if c == chunks - 1:
                        last.then_inc(out_done, 1)
                return last

            def step_unit(n, e, tb, c, rows, before_unit, prep):
                up(n, e, tb, c, rows, 0)
                if prep:
                    turn_weights(prep[0], prep[1], 0, prep[2])
                up(n, e, tb, c, rows, 1)
                if prep:
                    turn_weights(prep[0], prep[1], 1, prep[2])
                down(*before_unit)
                if prep:
                    turn_weights(prep[0], prep[1], 2, prep[2])

            def token_block(e, tb, last_of_expert, next_left, prep_group):
                first_unit = e * UNITS + tb * NC
                blocks = e * TB + tb
                for c in range(1, NC + 1):
                    prep = None
                    if prep_group is not None and c - 1 < prep_group[1]:
                        prep = (prep_group[0], c - 1, prep_group[2])
                    before_unit = (first_unit + (c - 1), e, blocks, c - 1, P, NC)
                    if c < NC:
                        step_unit(first_unit + c, e, tb, c, P, before_unit, prep)
                    elif last_of_expert:
                        step_unit(first_unit + c, e + 1, 0, 0, LEFT if next_left else P, before_unit, prep)
                    else:
                        step_unit(first_unit + c, e, tb + 1, 0, P, before_unit, prep)

            def expert(e, last):
                with pe.Fori(0, TB - 1) as tb:
                    token_block(e, tb, False, False, None)
                token_block(e, TB - 1, True, last, (e + 1, TRIO, LEFT) if last else (e + 1, NC, P))

            pe.wait_ge(gatesT_ready, 2)
            up(0, 0, 0, 0, P, 0)
            up(0, 0, 0, 0, P, 1)
            with pe.Fori(0, GROUPS - 1) as e:
                expert(e, False)
            expert(GROUPS - 1, True)
            first_left = GROUPS * UNITS
            for n in range(1, TB * TRIO):
                step_unit(first_left + n, GROUPS, n // TRIO, n % TRIO, LEFT,
                          (first_left + n - 1, GROUPS, GROUPS * TB + (n - 1) // TRIO, (n - 1) % TRIO, LEFT, TRIO), None)
            n = TB * TRIO - 1
            down(first_left + n, GROUPS, GROUPS * TB + n // TRIO, n % TRIO, LEFT, TRIO)


_INS = ["x", "ctx_2048", "L0_xattn_ssm_kernel", "L0_xattn_D", "L0_ffn_sw1", "L0_ffn_sw2", "L0_ffn_sw3",
        "L0_ffn_ew1", "L0_ffn_ew2", "L0_ffn_ew3", "L0_ffn_wr"]


def kernel(**inputs):
    import numpy as _np
    import concourse.bacc as _bacc
    from concourse import mybir as _mybir
    from concourse.bass_utils import run_bass_kernel_spmd as _run

    nc = _bacc.Bacc("TRN2", target_bir_lowering=False, num_devices=1)
    arrays, args = {}, []
    for name in _INS:
        a = _np.ascontiguousarray(inputs[name])
        arrays[f"in_{name}_dram"] = a
        args.append(nc.dram_tensor(f"in_{name}_dram", a.shape, _mybir.dt.from_np(a.dtype), kind="ExternalInput").ap())
    out = nc.dram_tensor("out_0_dram", (BATCH, CH, L), _mybir.dt.float32, kind="ExternalOutput").ap()
    build(nc, *args, out)
    r = _run(nc, [arrays], core_ids=[0])
    return r.results[0]["out_0_dram"]
```

```python
from contextlib import ExitStack

import concourse.bass as bass
from concourse import mybir

F32 = mybir.dt.float32
F32R = mybir.dt.float32r
I32 = mybir.dt.int32
ALU = mybir.AluOpType
ACT = mybir.ActivationFunctionType
AX = mybir.AxisListType

P = 128
BATCH, CH, L = 8, 256, 512
HD = 8
HEADS = CH // HD
LB = L // P
TOK = BATCH * CH
TILES = TOK // P
HT = BATCH * HD
PAIRS = HT * HD
EXPERTS = 8
HID = L * 4 // 3
NC = -(-HID // P)
TB = TOK // 512
TOPK = 2
ST = 256
STEPS = (TOK * TOPK + EXPERTS * (ST - 1)) // ST
GROUPS = 1 + STEPS
SLOTS = STEPS * ST
JOBS = 3 * NC
STEP_JOBS = JOBS + ST // P
KROW = P + L
EPS = 1e-5


def positive(value):
    return not isinstance(value, int) or value > 0


def rows_of(c):
    return min(P, HID - c * P)


def first_job(group):
    return 0 if isinstance(group, int) and group == 0 else group * STEP_JOBS - (STEP_JOBS - JOBS)


def job_of(group, c, m):
    return 3 * c + m + (0 if isinstance(group, int) and group == 0 else (c >= 2) + (c >= 4))


PICKED_STEP = 12
X_JOB = {1: 6, 3: 13}


def build(nc, x, ctx_in, ssm_kernel, d_skip, sw1, sw2, sw3, ew1, ew2, ew3, wr, out):
    kpad = nc.dram_tensor("kpad", (HEADS, KROW), F32, kind="Internal").ap()
    yn_dram = nc.dram_tensor("yn_rows", (TOK, L), F32, kind="Internal").ap()
    token_of_slot = nc.dram_tensor("token_of_slot", (SLOTS, 1), I32, kind="Internal").ap()
    result_dram = nc.dram_tensor("result_by_slot", (SLOTS, L), F32, kind="Internal").ap()

    base = 16512
    place = {"at": base}

    def sb(name, shape, dt=F32, at=None):
        size = 4
        for n in shape[1:]:
            size *= n
        if at is None:
            at = place["at"]
            place["at"] = at + (size + 31) // 32 * 32
        return nc.alloc_sbuf_tensor_at(name, shape, dt, offset=at)

    acc = sb("acc", [P, TILES, L])
    x_hi = sb("x_hi", [P, LB, TOK], F32R)
    x_lo = sb("x_lo", [P, LB, TOK], F32R)
    stage = place["at"]
    w1_hi = sb("w1_hi", [P, NC, LB, P], F32R)
    w1_lo = sb("w1_lo", [P, NC, LB, P], F32R)
    w3_hi = sb("w3_hi", [P, NC, LB, P], F32R)
    w3_lo = sb("w3_lo", [P, NC, LB, P], F32R)
    w2_hi = sb("w2_hi", [P, NC, L], F32R)
    w2_lo = sb("w2_lo", [P, NC, L], F32R)
    h_hi = sb("h_hi", [P, 2, 512], F32R)
    h_lo = sb("h_lo", [P, 2, 512], F32R)
    silu_u = sb("silu_u", [P, 512])
    hidden = sb("hidden", [P, 512])
    stage_end = place["at"]
    raw_area = stage_end
    w1_raw = sb("w1_raw", [P, 2, L])
    w3_raw = sb("w3_raw", [P, 2, L])
    w2_raw = sb("w2_raw", [P, 2, LB, P])
    router_area = place["at"]
    tokens_raw = sb("tokens_raw", [P, 2, ST // P, L])
    router_end = place["at"]
    x_hi_at = stage - 2 * LB * TOK * 4
    row_bytes = TOK * 4
    step_hi = [sb(f"step_hi{i}", [P, LB, ST], F32R, at=x_hi_at + 2 * i * row_bytes) for i in range(2)]
    step_lo = [sb(f"step_lo{i}", [P, LB, ST], F32R, at=x_hi_at + (2 * i + 1) * row_bytes) for i in range(2)]
    x_lo_at = x_hi_at + LB * TOK * 4
    result = sb("result", [P, 2, ST // P, L], at=x_lo_at)
    chosen = sb("chosen", [P, 4, TOPK, L], at=x_lo_at + 2 * (ST // P) * L * 4)
    ident = sb("ident", [P, P])
    minus_half = sb("minus_half", [P, 1])
    stats = sb("stats", [P, 2, 6])
    moments = sb("moments", [P, 2, 2])
    var_eps = sb("var_eps", [P, 2])
    minus_mean = sb("minus_mean", [P, 2])
    rstd = sb("rstd", [P, 2])
    shift = sb("shift", [P, 2])
    wr_hi = sb("wr_hi", [P, LB, EXPERTS], F32R)
    wr_lo = sb("wr_lo", [P, LB, EXPERTS], F32R)
    logits = sb("logits", [P, TILES, EXPERTS])
    probs = sb("probs", [P, TILES, EXPERTS])
    rank = sb("rank", [P, TILES, EXPERTS])
    wr_rows_at = place["at"]
    picked = sb("picked", [P, TILES, EXPERTS])
    slot = sb("slot", [P, TILES, EXPERTS])
    upto = [sb(f"upto{i}", [P, TILES, EXPERTS]) for i in range(2)]
    wr_rows = sb("wr_rows", [EXPERTS, L], at=wr_rows_at)
    per_tile = sb("per_tile", [P, 3, TILES])
    gate = sb("gate", [P, TOPK, TILES])
    route = sb("route", [P, TILES, TOPK + 1], I32)
    route_now = sb("route_now", [P, TOPK + 1], I32)
    route_back = sb("route_back", [P, TOPK], I32)
    ids = sb("ids", [P, SLOTS // P], I32)
    ids_now = sb("ids_now", [P, 2, ST // P], I32)
    expert_of_step = sb("expert_of_step", [P, STEPS], I32)
    table_area = place["at"]
    table_end = 229368
    place["at"] = stage
    x_raw = sb("x_raw", [P, 2, L])
    c_raw = sb("c_raw", [P, 2, L])
    c_rev = sb("c_rev", [P, L])
    xn = sb("xn", [P, 2, L])
    yn = sb("yn", [P, L])
    qT = sb("qT", [P, 2, LB, P])
    cT = sb("cT", [P, 2, LB, P])
    t_raw = sb("t_raw", [P, 2, L])
    t_hi = sb("t_hi", [P, 2, L], F32R)
    t_lo = sb("t_lo", [P, 2, L], F32R)
    kv = sb("kv", [P, 2, PAIRS])
    kv_hi = sb("kv_hi", [P, 2, LB, PAIRS], F32R)
    kv_lo = sb("kv_lo", [P, 2, LB, PAIRS], F32R)
    scaled = sb("scaled", [P, 2, PAIRS])
    attnT = sb("attnT", [P, 2, LB, P])
    assert place["at"] <= stage_end, (place["at"], stage_end)
    krows = sb("krows", [HEADS, KROW], at=raw_area)
    d_col = sb("d_col", [HEADS, 1], at=raw_area + 4096)
    zero_ids = sb("zero_ids", [P, SLOTS // P], I32, at=raw_area + 4608)
    place["at"] = router_area
    logitsT = sb("logitsT", [EXPERTS, TB, 512])
    place["at"] = router_area
    larger = sb("larger", [P, TILES, EXPERTS, EXPERTS])
    equal = sb("equal", [P, TILES, EXPERTS, EXPERTS])
    assert place["at"] <= router_end
    place["at"] = table_area
    before = sb("before", [P, EXPERTS, EXPERTS])
    earlier = sb("earlier", [P, P])
    ones = sb("ones", [P, P])
    limits = sb("limits", [P, TOK // ST])
    step_no = sb("step_no", [P, STEPS])
    per_expert = sb("per_expert", [P, 2, EXPERTS])
    pairs8 = sb("pairs8", [P, EXPERTS, EXPERTS])
    assert place["at"] <= table_end, (place["at"], table_end)
    place["at"] = router_area
    by_step = sb("by_step", [P, STEPS, EXPERTS])
    step_expert = sb("step_expert", [P, STEPS])

    with ExitStack() as stack:
        def sem(name):
            return stack.enter_context(nc.semaphore(name))

        banks = [stack.enter_context(nc.psum_tensor(f"bank{i}", [P, 512], F32)) for i in range(8)]
        conv_ps = banks[0:4]
        q_ps, c_ps, attn_ps, yn_ps = banks[4], banks[5], banks[6], banks[7]
        out_ps, u_ps, v_ps, w_ps = banks[0:4], banks[4], banks[5], banks[6:8]
        wr_ps, router_ps = banks[6], banks[7]

        zeroed = sem("zeroed"); ident_ready = sem("ident_ready"); kern_in = sem("kern_in")
        kern_skip = sem("kern_skip"); kpad_written = sem("kpad_written")
        x_in = [sem(f"x_in{i}") for i in range(2)]
        c_in = [sem(f"c_in{i}") for i in range(2)]
        t_in = [sem(f"t_in{i}") for i in range(2)]
        ln_steps = sem("ln_steps"); rstd_ready = sem("rstd_ready"); shift_ready = sem("shift_ready")
        c_reversed = sem("c_reversed"); xn_ready = sem("xn_ready")
        q_turned = sem("q_turned"); c_turned = sem("c_turned")
        qT_ready = sem("qT_ready"); cT_ready = sem("cT_ready")
        t_hi_ready = sem("t_hi_ready"); t_lo_ready = sem("t_lo_ready")
        kv_ready = sem("kv_ready"); kv_hi_ready = sem("kv_hi_ready"); kv_lo_ready = sem("kv_lo_ready")
        conv_done = sem("conv_done"); scaled_ready = sem("scaled_ready"); attn_ready = sem("attn_ready")
        attn_turned = sem("attn_turned"); acc_written = sem("acc_written"); yn_ready = sem("yn_ready")
        yn_turned = sem("yn_turned"); x_hi_ready = sem("x_hi_ready"); x_lo_ready = sem("x_lo_ready")
        yn_stored = sem("yn_stored")
        wr_in = sem("wr_in"); wr_turned = sem("wr_turned"); wr_hi_ready = sem("wr_hi_ready")
        wr_lo_ready = sem("wr_lo_ready"); logits_done = sem("logits_done")
        logitsT_ready = sem("logitsT_ready"); logits_turned = sem("logits_turned")
        masks_filled = sem("masks_filled"); masks_ready = sem("masks_ready")
        route_steps = sem("route_steps"); exp_ready = sem("exp_ready"); counted = sem("counted")
        zero_ids_ready = sem("zero_ids_ready"); ids_cleared = sem("ids_cleared")
        route_ready = sem("route_ready"); route_copied = sem("route_copied")
        ids_written = sem("ids_written"); ids_in = sem("ids_in"); ids_copied = sem("ids_copied")
        w_in = [sem(f"w_in{i}") for i in range(2)]
        tokens_in = [sem(f"tokens_in{i}") for i in range(2)]
        w_turned = sem("w_turned"); w_hi_ready = sem("w_hi_ready"); w_lo_ready = sem("w_lo_ready")
        u_done = sem("u_done"); v_done = sem("v_done"); silu_ready = sem("silu_ready")
        hidden_ready = sem("hidden_ready")
        h_hi_ready = sem("h_hi_ready"); h_lo_ready = sem("h_lo_ready")
        out_done = sem("out_done"); out_read = sem("out_read")
        result_stored = [sem(f"result_stored{i}") for i in range(2)]
        back_copied = sem("back_copied"); chosen_in = [sem(f"chosen_in{i}") for i in range(4)]
        chosen_added = sem("chosen_added"); out_written = sem("out_written")

        x_heads = x.rearrange("b (t s j) l -> t s b j l", s=2, j=HD)
        c_heads = ctx_in.rearrange("b (t s j) l -> t s b j l", s=2, j=HD)
        out_heads = out.rearrange("b (t s j) l -> t s b j l", s=2, j=HD)

        def split3(hi_a, lo_a, hi_b, lo_b):
            return ((hi_a, hi_b), (hi_a, lo_b), (lo_a, hi_b))

        def unit_no(step, c):
            return TB * NC + step * NC + c

        block = stack.enter_context(nc.Block())

        @block.sync
        def _(sp):
            sp.dma_start(krows[:, P:KROW], ssm_kernel).then_inc(kern_in, 16)
            sp.dma_start(d_col[:, :], d_skip.rearrange("(h o) -> h o", o=1)).then_inc(kern_in, 16)

            def load_tile(t, p):
                if not (isinstance(t, int) and t < 2):
                    used = sp.to_reg(t - 1)
                    sp.wait_ge(xn_ready, used)
                    sp.wait_ge(c_reversed, used)
                for s in range(2):
                    sp.dma_start(acc[s * HT:(s + 1) * HT, bass.ds(t, 1), :].rearrange("p o l -> p (o l)"),
                                 x_heads[bass.ds(t, 1), s, :, :, :].rearrange("o b j l -> (o b) j l")
                                 ).then_inc(x_in[p], 16)
                    for raw, heads, landed in ((x_raw, x_heads, x_in), (c_raw, c_heads, c_in)):
                        sp.dma_start(raw[s * HT:(s + 1) * HT, p, :],
                                     heads[bass.ds(t, 1), s, :, :, :].rearrange("o b j l -> (o b) j l")
                                     ).then_inc(landed[p], 16)

            def load_table(t, s):
                if not (isinstance(t, int) and t < 1):
                    used = sp.to_reg(2 * t + s - 1)
                    sp.wait_ge(t_lo_ready, used)
                sp.dma_start(t_raw[:, s, :],
                             bass.AP(kpad.tensor, t * (2 * KROW) + (s * KROW + 1), [[1, P], [1, L]])
                             ).then_inc(t_in[s], 16)

            load_tile(0, 0)
            load_tile(1, 1)
            sp.wait_ge(kern_skip, 1)
            sp.wait_ge(zeroed, 2)
            sp.dma_start(kpad, krows[:, :]).then_inc(kpad_written, 16)
            sp.wait_ge(kpad_written, 16)
            load_table(0, 0)
            load_table(0, 1)
            load_table(1, 0)
            load_table(1, 1)
            def store_yn(t):
                done = t + 1 if isinstance(t, int) else sp.to_reg(t + 1)
                sp.wait_ge(yn_ready, done)
                sp.dma_start(yn_dram.rearrange("(t p) l -> t p l", p=P)[bass.ds(t, 1), :, :
                                                                       ].rearrange("o p l -> (o p) l"),
                             yn[:, :]).then_inc(yn_stored, 16)

            sp.wait_ge(zero_ids_ready, 1)
            sp.dma_start(token_of_slot.rearrange("(p c) o -> p (c o)", p=P), zero_ids[:, :]).then_inc(ids_cleared, 16)
            for t in range(2, 4):
                load_tile(t, t % 2)
                load_table(t, 0)
                load_table(t, 1)
                if t >= 3:
                    store_yn(t - 3)
            with sp.Fori(2, TILES // 2) as half:
                for p in range(2):
                    load_tile(2 * half + p, p)
                    load_table(2 * half + p, 0)
                    load_table(2 * half + p, 1)
                    store_yn(2 * half + (p - 3))

            def load_chunk(group, c, w1, w3, w2):
                rows = rows_of(c)
                if not (isinstance(group, int) and group == 0 and c < 2):
                    if isinstance(group, int) and group == 0:
                        turned = 3 * c - 3
                    elif c < 2:
                        turned = group * STEP_JOBS + (3 * c - 5)
                    else:
                        turned = first_job(group) + (job_of(group, c - 2, 2) + 1)
                    if not isinstance(turned, int):
                        turned = sp.to_reg(turned)
                    sp.wait_ge(w_turned, turned)
                for raw, w in ((w1_raw, w1), (w3_raw, w3)):
                    sp.dma_start(raw[0:rows, c % 2, :], w[c * P:c * P + rows, :]).then_inc(w_in[c % 2], 16)
                sp.dma_start(w2_raw[:, c % 2, :, 0:rows],
                             w2[:, c * P:c * P + rows].rearrange("(d p) h -> p d h", p=P)
                             ).then_inc(w_in[c % 2], 16)

            sp.dma_start(wr_rows[:, :], wr).then_inc(wr_in, 16)
            for c in range(NC):
                if c == 2:
                    for t in range(TILES - 3, TILES):
                        store_yn(t)
                load_chunk(0, c, sw1, sw3, sw2)

            sp.wait_ge(ids_written, 16 * TOPK * TILES)
            sp.dma_start(ids[:, :], token_of_slot.rearrange("(c p) o -> p (c o)", p=P),
                         allow_slow_non_contiguous=True).then_inc(ids_in, 16)

            results = result_dram.rearrange("(k i p) l -> k p i l", i=ST // P, p=P)

            def store_result(step, slot_no, nth):
                copied = 4 * TB + 2 * step + 2
                sp.wait_ge(out_read, copied if isinstance(copied, int) else sp.to_reg(copied))
                sp.dma_start(results[bass.ds(step, 1), :, :, :].rearrange("o p i l -> (o p) i l"),
                             result[:, slot_no, :, :]).then_inc(result_stored[slot_no], 16)

            def load_step(step, back):
                expert = sp.value_load(expert_of_step[0:1, bass.ds(step, 1)], min_val=0, max_val=EXPERTS - 1)
                w1, w3, w2 = (w[bass.ds(expert, 1), :, :].rearrange("o r c -> (o r) c") for w in (ew1, ew3, ew2))
                for c in range(NC):
                    load_chunk(step + 1, c, w1, w3, w2)
                    if c == 2 and back is not None:
                        store_result(step - 2, back, None)

            load_step(0, None)
            load_step(1, None)
            load_step(2, 0)
            with sp.Fori(1, (STEPS - 1) // 2) as half:
                load_step(2 * half + 1, 1)
                load_step(2 * half + 2, 0)
            store_result(STEPS - 2, (STEPS - 2) % 2, None)
            store_result(STEPS - 1, (STEPS - 1) % 2, None)

            with sp.Fori(0, TILES) as t:
                tile_added = sp.to_reg(TOPK * t + TOPK)
                sp.wait_ge(chosen_added, tile_added)
                for s in range(2):
                    sp.dma_start(out_heads[bass.ds(t, 1), s, :, :, :].rearrange("o b j l -> (o b) j l"),
                                 acc[s * HT:(s + 1) * HT, bass.ds(t, 1), :].rearrange("p o l -> p (o l)")
                                 ).then_inc(out_written, 16)
            sp.wait_ge(out_written, 16 * 2 * TILES)

        @block.gpsimd
        def _(pool):
            nc.gpsimd.memset(krows[:, 0:P], 0.0).then_inc(zeroed, 1)
            nc.gpsimd.memset(minus_half[:, :], -0.5).then_inc(zeroed, 1)
            nc.gpsimd.memset(ident[:, :], 0.0).then_inc(zeroed, 1)
            nc.gpsimd.memset(zero_ids[:, :], 0).then_inc(zero_ids_ready, 1)
            pool.wait_ge(zeroed, 3)
            nc.gpsimd.affine_select(out=ident[:, :], in_=ident[:, :], compare_op=ALU.not_equal, fill=1.0,
                                    base=0, pattern=[[-1, P]], channel_multiplier=1).then_inc(ident_ready, 1)

            nc.gpsimd.memset(before[:, :, :], 1.0).then_inc(masks_filled, 1)
            nc.gpsimd.memset(earlier[:, :], 1.0).then_inc(masks_filled, 1)
            nc.gpsimd.memset(ones[:, :], 1.0).then_inc(masks_ready, 1)
            pool.wait_ge(masks_filled, 2)
            nc.gpsimd.affine_select(out=before[:, :, :], in_=before[:, :, :], compare_op=ALU.is_gt, fill=0.0,
                                    base=0, pattern=[[1, EXPERTS], [-1, EXPERTS]], channel_multiplier=0
                                    ).then_inc(masks_ready, 1)
            nc.gpsimd.affine_select(out=earlier[:, :], in_=earlier[:, :], compare_op=ALU.is_gt, fill=0.0,
                                    base=0, pattern=[[1, P]], channel_multiplier=-1).then_inc(masks_ready, 1)
            nc.gpsimd.iota(limits[:, :], [[ST, TOK // ST]], base=0, channel_multiplier=0,
                           allow_small_or_imprecise_dtypes=True).then_inc(masks_ready, 1)
            nc.gpsimd.iota(step_no[:, :], [[1, STEPS]], base=0, channel_multiplier=0,
                           allow_small_or_imprecise_dtypes=True).then_inc(masks_ready, 1)
            nc.gpsimd.iota(route[:, :, TOPK:TOPK + 1], [[P, TILES], [1, 1]], base=0, channel_multiplier=1
                           ).then_inc(route_ready, 1)

            def ln_tail(n, k):
                pool.wait_ge(ln_steps, 4 * n)
                nc.gpsimd.tensor_tensor(rstd[:, k:k + 1], var_eps[:, k:k + 1], minus_half[:, :], ALU.pow
                                        ).then_inc(rstd_ready, 1)
                pool.wait_ge(rstd_ready, n)
                nc.gpsimd.tensor_tensor(shift[:, k:k + 1], minus_mean[:, k:k + 1], rstd[:, k:k + 1], ALU.mult
                                        ).then_inc(shift_ready, 1)

            def split_table(g, s):
                pool.wait_ge(t_hi_ready, g + 1)
                if not (isinstance(g, int) and g < 2):
                    pool.wait_ge(conv_done, LB * (g - 1))
                nc.gpsimd.tensor_tensor(t_lo[:, s, :], t_raw[:, s, :], t_hi[:, s, :].bitcast(F32),
                                        ALU.subtract).then_inc(t_lo_ready, 1)

            def products(g, s, p):
                for k in range(LB):
                    n = g * LB + k
                    if k == 0:
                        pool.wait_ge(cT_ready, (g - s + 2) // 2 if isinstance(g, int) else tile_of[0] + 1)
                    if not (isinstance(n, int) and n < 2):
                        pool.wait_ge(kv_lo_ready, n - 1)
                    one = cT[:, p, k, s * HT:(s + 1) * HT].rearrange("p (b j) -> p b j", j=HD)
                    nc.gpsimd.tensor_tensor(kv[:, k % 2, :].rearrange("p (b j i) -> p b j i", j=HD, i=HD),
                                            one.unsqueeze(3).broadcast_to([P, BATCH, HD, HD]),
                                            one.unsqueeze(2).broadcast_to([P, BATCH, HD, HD]),
                                            ALU.mult).then_inc(kv_ready, 1)

            tile_of = [None]
            ln_tail(1, 0)
            split_table(0, 0)
            products(0, 0, 0)

            def step(s, p):
                last = isinstance(s, int) and s == TILES - 1
                first = isinstance(s, int) and s == 0
                if not last:
                    ln_tail(2 if first else 2 * s + 1, 0)
                split_table(2 * s + 1, 1)
                tile_of[0] = s
                products(2 * s + 1, 1, p)
                if not first:
                    ln_tail(2 * s + 1 if last else 2 * s + 2, 1)
                if not last:
                    split_table(2 * s + 2, 0)
                    tile_of[0] = s + 1
                    products(2 * s + 2, 0, 1 - p)

            step(0, 0)
            step(1, 1)
            with pool.Fori(1, TILES // 2 - 1) as half:
                step(2 * half, 0)
                step(2 * half + 1, 1)
            step(TILES - 2, 0)
            step(TILES - 1, 1)
            ln_tail(2 * TILES, 1)

            pool.wait_ge(route_ready, 5)
            pool.wait_ge(ids_cleared, 16)
            with pool.Fori(0, TILES) as t:
                nc.gpsimd.tensor_copy(route_now[:, :], route[:, bass.ds(t, 1), :].rearrange("p o r -> p (o r)")
                                      ).then_inc(route_copied, 1)
                copied, free = pool.to_reg(t + 1), pool.to_reg(t * (16 * TOPK) + 16)
                for r in range(TOPK):
                    pool.wait_ge(route_ready, 5)
                    if r == 0:
                        pool.wait_ge(route_copied, copied)
                    else:
                        pool.wait_ge(ids_written, free)
                    pool.indirect_dma_start(token_of_slot, bass.IndirectOffsetOnAxis(route_now[:, r:r + 1], 0),
                                            route_now[:, TOPK:TOPK + 1], None).then_inc(ids_written, 16)
                written = pool.to_reg(t * (16 * TOPK) + 16 * TOPK)
                pool.wait_ge(ids_written, written)

            pool.wait_ge(ids_in, 16)
            pool.wait_ge(yn_stored, 16 * TILES)
            pool.wait_ge(route_ready, 5)

            def gather_tokens(step, p, before_it):
                if not isinstance(before_it, int):
                    before_it = pool.to_reg(before_it * 16)
                    pool.wait_ge(ids_in, 16)
                    pool.wait_ge(tokens_in[p], before_it)
                elif before_it:
                    pool.wait_ge(tokens_in[p], 16 * before_it)
                nc.gpsimd.tensor_copy(ids_now[:, p, :], ids[:, bass.ds(step * (ST // P), ST // P)]).then_inc(ids_copied, 1)
                copied, free = step + 1, first_job(step) + (X_JOB[3] + 1 - STEP_JOBS)
                if not isinstance(step, int):
                    copied, free = pool.to_reg(copied), pool.to_reg(free)
                pool.wait_ge(ids_in, 16)
                pool.wait_ge(ids_copied, copied)
                if not (isinstance(step, int) and step < 2):
                    pool.wait_ge(w_turned, free)
                for i in range(ST // P):
                    pool.indirect_dma_start(tokens_raw[:, p, i, :], None, yn_dram,
                                            bass.IndirectOffsetOnAxis(ids_now[:, p, i:i + 1], 0)
                                            ).then_inc(tokens_in[p], 16)

            gather_tokens(0, 0, 0)
            gather_tokens(1, 1, 0)
            with pool.Fori(1, STEPS // 2) as half:
                gather_tokens(2 * half, 0, (ST // P) * half)
                gather_tokens(2 * half + 1, 1, (ST // P) * half)
            gather_tokens(STEPS - 1, 0, (ST // P) * (STEPS // 2))

            for i in range(2):
                pool.wait_ge(result_stored[i], 16 * ((STEPS + 1 - i) // 2))
            for t in range(TILES):
                if t >= 1:
                    pool.wait_ge(chosen_in[(t - 1) % 4], 16 * TOPK * ((t - 1) // 4 + 1))
                nc.gpsimd.tensor_copy(route_back[:, :], route[:, t, 0:TOPK]).then_inc(back_copied, 1)
                pool.wait_ge(back_copied, t + 1)
                if t >= 4:
                    pool.wait_ge(chosen_added, TOPK * (t - 3))
                for r in range(TOPK):
                    pool.indirect_dma_start(chosen[:, t % 4, r, :], None, result_dram,
                                            bass.IndirectOffsetOnAxis(route_back[:, r:r + 1], 0)
                                            ).then_inc(chosen_in[t % 4], 16)

        @block.scalar
        def _(act):
            def reverse_ctx(t, p, use):
                act.wait_ge(c_in[p], use)
                if not (isinstance(t, int) and t < 1):
                    act.wait_ge(c_turned, t)
                nc.scalar.activation(c_rev[:, :], c_raw[:, p, ::-1], ACT.Copy).then_inc(c_reversed, 1)

            def normalise_x(t, p, n):
                act.wait_ge(shift_ready, n)
                if not (isinstance(t, int) and t < 2):
                    act.wait_ge(q_turned, t - 1)
                nc.scalar.activation(xn[:, p, :], x_raw[:, p, :], ACT.Identity, bias=shift[:, 0:1],
                                     scale=rstd[:, 0:1]).then_inc(xn_ready, 1)

            def round_table(g, s, use):
                act.wait_ge(t_in[s], use)
                if not (isinstance(g, int) and g < 2):
                    act.wait_ge(conv_done, LB * (g - 1))
                nc.scalar.activation(t_hi[:, s, :], t_raw[:, s, :], ACT.Copy).then_inc(t_hi_ready, 1)

            def round_products(g, s):
                for k in range(LB):
                    act.wait_ge(kv_ready, g * LB + (k + 1))
                    if k == 0 and not (isinstance(g, int) and g < 2):
                        act.wait_ge(conv_done, LB * (g - 1))
                    nc.scalar.activation(kv_hi[:, s, k, :], kv[:, k % 2, :], ACT.Copy).then_inc(kv_hi_ready, 1)

            def keep_turned(t, p):
                act.wait_ge(q_turned, t + 1)
                if not (isinstance(t, int) and t < 2):
                    act.wait_ge(scaled_ready, 2 * LB * (t - 1))
                    act.wait_ge(kv_ready, 2 * LB * (t - 1))
                nc.scalar.activation(qT[:, p, :, :].rearrange("p k c -> p (k c)"), q_ps[:, :], ACT.Copy
                                     ).then_inc(qT_ready, 1)
                act.wait_ge(c_turned, t + 1)
                nc.scalar.activation(cT[:, p, :, :].rearrange("p k c -> p (k c)"), c_ps[:, :], ACT.Copy
                                     ).then_inc(cT_ready, 1)

            def normalise_y(t, n):
                act.wait_ge(shift_ready, n)
                if not (isinstance(t, int) and t < 1):
                    act.wait_ge(yn_turned, t)
                    act.wait_ge(yn_stored, 16 * t)
                nc.scalar.activation(yn[:, :].unsqueeze(1), acc[:, bass.ds(t, 1), :], ACT.Identity,
                                     bias=shift[:, 1:2], scale=rstd[:, 1:2]).then_inc(yn_ready, 1)

            def round_x(t):
                act.wait_ge(yn_turned, t + 1)
                nc.scalar.activation(x_hi[:, :, bass.ds(t * P, P)], yn_ps[:, :].rearrange("p (k c) -> p k c", c=P),
                                     ACT.Copy).then_inc(x_hi_ready, 1)

            reverse_ctx(0, 0, 32)
            normalise_x(0, 0, 1)
            round_table(0, 0, 16)
            keep_turned(0, 0)
            round_products(0, 0)

            def step(s, p, nth):
                last = isinstance(s, int) and s == TILES - 1
                first = isinstance(s, int) and s == 0
                if not last:
                    fills = 32 * (nth + p) + 32
                    reverse_ctx(s + 1, 1 - p, fills)
                    normalise_x(s + 1, 1 - p, 2 if first else 2 * s + 1)
                if not (isinstance(s, int) and s < 2):
                    round_x(s - 2)
                round_table(2 * s + 1, 1, 16 * s + 16)
                round_products(2 * s + 1, 1)
                if not last:
                    keep_turned(s + 1, 1 - p)
                    round_table(2 * s + 2, 0, 16 * s + 32)
                if not first:
                    normalise_y(s - 1, 2 * s + 1 if last else 2 * s + 2)
                if not last:
                    round_products(2 * s + 2, 0)

            step(0, 0, 0)
            step(1, 1, 0)
            with act.Fori(1, TILES // 2 - 1) as half:
                step(2 * half, 0, half)
                step(2 * half + 1, 1, half)
            step(TILES - 2, 0, TILES // 2 - 1)
            step(TILES - 1, 1, TILES // 2 - 1)
            round_x(TILES - 2)
            normalise_y(TILES - 1, 2 * TILES)
            round_x(TILES - 1)

            def weight_block(c, m, bank, w1, w3, w2):
                rows = rows_of(c)
                if m < 2:
                    return (w1, w3)[m][:, c, :, 0:rows], bank[:, :].rearrange("p (k c) -> p k c", c=P)[:, :, 0:rows]
                return w2[0:rows, c, :], bank[0:rows, :]

            def round_weights(group, c, m):
                q = job_of(group, c, m)
                act.wait_ge(w_turned, first_job(group) + (q + 1))
                dst, src = weight_block(c, m, w_ps[q % 2], w1_hi, w3_hi, w2_hi)
                nc.scalar.activation(dst, src, ACT.Copy).then_inc(w_hi_ready, 1)

            def round_tokens(group, i, p):
                q = X_JOB[1 + 2 * i]
                act.wait_ge(w_turned, first_job(group) + (q + 1))
                nc.scalar.activation(step_hi[p][:, :, i * P:(i + 1) * P],
                                     w_ps[q % 2][:, :].rearrange("p (k c) -> p k c", c=P), ACT.Copy
                                     ).then_inc(w_hi_ready, 1)

            act.wait_ge(yn_stored, 16 * TILES)
            for c in range(NC):
                for m in range(3):
                    round_weights(0, c, m)

            act.wait_ge(wr_turned, 1)
            nc.scalar.activation(wr_hi[:, :, :], wr_ps[:, 0:LB * EXPERTS].rearrange("p (k e) -> p k e", e=EXPERTS),
                                 ACT.Copy).then_inc(wr_hi_ready, 1)
            for tb in range(TB):
                act.wait_ge(logits_done, tb + 1)
                nc.scalar.activation(logitsT[:, tb, :], banks[tb][0:EXPERTS, :], ACT.Copy).then_inc(logitsT_ready, 1)
            act.wait_ge(route_steps, 3)
            nc.scalar.activation(probs[:, :, :], logits[:, :, :], ACT.Exp).then_inc(exp_ready, 1)

            def unit(n, c, width, turn_group=None, turn_c=None, p=None):
                rows = rows_of(c)
                act.wait_ge(u_done, n + 1)
                if positive(n):
                    act.wait_ge(hidden_ready, n)
                nc.scalar.activation(silu_u[0:rows, 0:width], u_ps[0:rows, 0:width], ACT.Silu).then_inc(silu_ready, 1)
                if turn_group is not None:
                    round_weights(turn_group, turn_c, 0)
                    round_weights(turn_group, turn_c, 1)
                act.wait_ge(hidden_ready, n + 1)
                nc.scalar.activation(h_hi[0:rows, c % 2, 0:width], hidden[0:rows, 0:width], ACT.Copy
                                     ).then_inc(h_hi_ready, 1)
                if turn_group is not None:
                    round_weights(turn_group, turn_c, 2)
                    if turn_c in X_JOB:
                        round_tokens(turn_group, turn_c // 2, p)

            def keep_result(step, p):
                for i in range(ST // P):
                    act.wait_ge(out_done, 4 * TB + 2 * step + (i + 1))
                    if i == 0 and not (isinstance(step, int) and step < 2):
                        act.wait_ge(result_stored[p], result_fills)
                    nc.scalar.activation(result[:, p, i, :], out_ps[2 * p + i][:, :], ACT.Copy).then_inc(out_read, 1)

            unit(0, 0, 512)
            with act.Fori(0, TB - 1) as tb:
                for c in range(1, NC + 1):
                    unit(tb * NC + c, c % NC, 512)
            for c in range(1, NC):
                unit((TB - 1) * NC + c, c, 512, 1, c - 1, 0)
            unit(TB * NC, 0, ST, 1, NC - 1, 0)

            def step(k, p):
                for c in range(1, NC + 1):
                    unit(unit_no(k, c), c % NC, ST, k + 2, c - 1, 1 - p)
                keep_result(k, p)

            result_fills = 0
            act.wait_ge(out_read, 4 * TB)
            step(0, 0)
            step(1, 1)
            with act.Fori(1, (STEPS - 1) // 2) as half:
                result_fills = half * 16
                step(2 * half, 0)
                step(2 * half + 1, 1)
            result_fills = 16 * ((STEPS - 1) // 2)
            for c in range(1, NC):
                unit(unit_no(STEPS - 1, c), c, ST)
            keep_result(STEPS - 1, 0)

        @block.vector
        def _(dve):
            dve.wait_ge(kern_in, 32)
            nc.vector.tensor_tensor(krows[:, P:P + 1], krows[:, P:P + 1], d_col[:, :], ALU.add).then_inc(kern_skip, 1)

            def moments_of(src, n, k):
                stats_done = 4 * n - 3 if isinstance(n, int) else dve.to_reg(4 * n - 3)
                nc.vector.bn_stats(stats[:, k, :], src).then_inc(ln_steps, 1)
                dve.wait_ge(kern_in, 32)
                dve.wait_ge(ln_steps, stats_done)
                nc.vector.bn_aggr(moments[:, k, :], stats[:, k, :]).then_inc(ln_steps, 1)
                dve.wait_ge(ln_steps, 4 * n - 2)
                nc.vector.tensor_scalar(var_eps[:, k:k + 1], moments[:, k, 1:2], EPS, None, ALU.add
                                        ).then_inc(ln_steps, 1)
                nc.vector.tensor_scalar(minus_mean[:, k:k + 1], moments[:, k, 0:1], -1.0, None, ALU.mult
                                        ).then_inc(ln_steps, 1)

            def moments_x(t, p, n, use):
                if not isinstance(t, int):
                    t, use = dve.to_reg(t), dve.to_reg(use)
                dve.wait_ge(kern_in, 32)
                dve.wait_ge(x_in[p], use)
                if not (isinstance(t, int) and t < 1):
                    dve.wait_ge(xn_ready, t)
                moments_of(x_raw[:, p, :], n, 0)

            def split_block(g, s, k):
                dve.wait_ge(kv_hi_ready, g * LB + (k + 1))
                nc.vector.tensor_tensor(kv_lo[:, s, k, :], kv[:, k % 2, :], kv_hi[:, s, k, :].bitcast(F32),
                                        ALU.subtract).then_inc(kv_lo_ready, 1)

            def contract(g, s, p, k, tile):
                n = g * LB + (k + 1)
                dve.wait_ge(conv_done, n)
                if k == 0 and s == 0:
                    dve.wait_ge(qT_ready, tile + 1)
                q = qT[:, p, k, s * HT:(s + 1) * HT].rearrange("p (b i) -> p b i", i=HD)
                nc.vector.tensor_tensor(scaled[:, k % 2, :].rearrange("p (b j i) -> p b j i", j=HD, i=HD),
                                        conv_ps[k][:, :].rearrange("p (b j i) -> p b j i", j=HD, i=HD),
                                        q.unsqueeze(2).broadcast_to([P, BATCH, HD, HD]), ALU.mult
                                        ).then_inc(scaled_ready, 1)
                if k == 0 and s == 0 and not (isinstance(tile, int) and tile < 2):
                    dve.wait_ge(attn_turned, tile - 1)
                dve.wait_ge(scaled_ready, n)
                nc.vector.tensor_reduce(attnT[:, p, k, s * HT:(s + 1) * HT],
                                        scaled[:, k % 2, :].rearrange("p (n i) -> p n i", i=HD), AX.X, ALU.add
                                        ).then_inc(attn_ready, 1)

            def add_residual(t, p, n):
                dve.wait_ge(attn_turned, t + 1)
                nc.vector.tensor_tensor(acc[:, bass.ds(t, 1), :], attn_ps[:, :].unsqueeze(1),
                                        acc[:, bass.ds(t, 1), :], ALU.add).then_inc(acc_written, 1)
                dve.wait_ge(kern_in, 32)
                dve.wait_ge(acc_written, t + 1)
                if not (isinstance(t, int) and t < 1):
                    dve.wait_ge(yn_ready, t)
                moments_of(acc[:, bass.ds(t, 1), :], n, 1)

            def split_x(t):
                dve.wait_ge(x_hi_ready, t + 1)
                nc.vector.tensor_tensor(x_lo[:, :, bass.ds(t * P, P)], yn_ps[:, :].rearrange("p (k c) -> p k c", c=P),
                                        x_hi[:, :, bass.ds(t * P, P)].bitcast(F32), ALU.subtract
                                        ).then_inc(x_lo_ready, 1)

            moments_x(0, 0, 1, 64)
            for k in range(LB):
                split_block(0, 0, k)

            def step(s, p, nth):
                last = isinstance(s, int) and s == TILES - 1
                first = isinstance(s, int) and s == 0
                if not last:
                    moments_x(s + 1, 1 - p, 2 if first else 2 * s + 1, 64 * (nth + p) + 64)
                for k in range(LB):
                    split_block(2 * s + 1, 1, k)
                    contract(2 * s, 0, p, k, s)
                if not (isinstance(s, int) and s < 2):
                    split_x(s - 2)
                if not first:
                    add_residual(s - 1, 1 - p, 2 * s + 1 if last else 2 * s + 2)
                for k in range(LB):
                    if not last:
                        split_block(2 * s + 2, 0, k)
                    contract(2 * s + 1, 1, p, k, s)

            step(0, 0, 0)
            step(1, 1, 0)
            with dve.Fori(1, TILES // 2 - 1) as half:
                step(2 * half, 0, half)
                step(2 * half + 1, 1, half)
            step(TILES - 2, 0, TILES // 2 - 1)
            step(TILES - 1, 1, TILES // 2 - 1)
            split_x(TILES - 2)
            add_residual(TILES - 1, 1, 2 * TILES)
            split_x(TILES - 1)

            def split_weights(group, c, m):
                q = job_of(group, c, m)
                rows = rows_of(c)
                bank = w_ps[q % 2]
                dve.wait_ge(w_hi_ready, first_job(group) + (q + 1))
                if m < 2:
                    dst = (w1_lo, w3_lo)[m][:, c, :, 0:rows]
                    hi = (w1_hi, w3_hi)[m][:, c, :, 0:rows]
                    src = bank[:, :].rearrange("p (k c) -> p k c", c=P)[:, :, 0:rows]
                else:
                    dst, hi, src = w2_lo[0:rows, c, :], w2_hi[0:rows, c, :], bank[0:rows, :]
                nc.vector.tensor_tensor(dst, src, hi.bitcast(F32), ALU.subtract).then_inc(w_lo_ready, 1)

            def split_tokens(group, i, p):
                q = X_JOB[1 + 2 * i]
                dve.wait_ge(w_hi_ready, first_job(group) + (q + 1))
                mine = slice(i * P, (i + 1) * P)
                nc.vector.tensor_tensor(step_lo[p][:, :, mine], w_ps[q % 2][:, :].rearrange("p (k c) -> p k c", c=P),
                                        step_hi[p][:, :, mine].bitcast(F32), ALU.subtract).then_inc(w_lo_ready, 1)

            for c in range(NC):
                for m in range(3):
                    split_weights(0, c, m)

            dve.wait_ge(wr_hi_ready, 1)
            nc.vector.tensor_tensor(wr_lo[:, :, :], wr_ps[:, 0:LB * EXPERTS].rearrange("p (k e) -> p k e", e=EXPERTS),
                                    wr_hi[:, :, :].bitcast(F32), ALU.subtract).then_inc(wr_lo_ready, 1)
            by_tile = [P, TILES, EXPERTS]
            pairwise = [P, TILES, EXPERTS, EXPERTS]
            top, total, inverse = (per_tile[:, i, :] for i in range(3))
            done = [0]

            def chained(instruction):
                done[0] += 1
                instruction.then_inc(route_steps, 1)
                dve.wait_ge(route_steps, done[0])

            dve.wait_ge(masks_ready, 5)
            dve.wait_ge(logits_turned, 1)
            chained(nc.vector.tensor_copy(logits[:, :, :], router_ps[:, 128:256].rearrange("p (t e) -> p t e", e=EXPERTS)))
            chained(nc.vector.tensor_reduce(top, logits[:, :, :], AX.X, ALU.max))
            chained(nc.vector.tensor_tensor(logits[:, :, :], logits[:, :, :], top.unsqueeze(2).broadcast_to(by_tile),
                                            ALU.subtract))
            dve.wait_ge(exp_ready, 1)
            chained(nc.vector.tensor_reduce(total, probs[:, :, :], AX.X, ALU.add))
            chained(nc.vector.reciprocal(inverse, total))
            chained(nc.vector.tensor_tensor(probs[:, :, :], probs[:, :, :], inverse.unsqueeze(2).broadcast_to(by_tile),
                                            ALU.mult))
            other = probs[:, :, :].unsqueeze(2).broadcast_to(pairwise)
            mine = probs[:, :, :].unsqueeze(3).broadcast_to(pairwise)
            chained(nc.vector.tensor_tensor(larger[:, :, :, :], other, mine, ALU.is_gt))
            chained(nc.vector.tensor_tensor(equal[:, :, :, :], other, mine, ALU.is_equal))
            chained(nc.vector.tensor_tensor(equal[:, :, :, :], equal[:, :, :, :],
                                            before[:, :, :].unsqueeze(1).broadcast_to(pairwise), ALU.mult))
            chained(nc.vector.tensor_tensor(larger[:, :, :, :], larger[:, :, :, :], equal[:, :, :, :], ALU.add))
            chained(nc.vector.tensor_reduce(rank[:, :, :], larger[:, :, :, :], AX.X, ALU.add))
            chained(nc.vector.tensor_scalar(picked[:, :, :], rank[:, :, :], TOPK - 0.5, None, ALU.is_lt))
            picked_at = done[0]
            assert picked_at == PICKED_STEP

            def slots():
                dve.wait_ge(counted, 1)
                within = router_ps[:, 256:384].rearrange("p (t e) -> p t e", e=EXPERTS)
                in_tile = router_ps[:, 384:512].rearrange("p (t e) -> p t e", e=EXPERTS)
                chained(nc.vector.tensor_copy(upto[0][:, :, :], in_tile))
                a = 0
                for d in (1, 2, 4, 8):
                    chained(nc.vector.tensor_copy(upto[1 - a][:, 0:d, :], upto[a][:, 0:d, :]))
                    chained(nc.vector.tensor_tensor(upto[1 - a][:, d:, :], upto[a][:, d:, :], upto[a][:, :TILES - d, :],
                                                    ALU.add))
                    a = 1 - a
                all_picks = upto[a][:, TILES - 1, :]
                steps_of, first_step = per_expert[:, 0, :], per_expert[:, 1, :]
                chained(nc.vector.tensor_tensor(pairs8[:, :, :], all_picks.unsqueeze(2).broadcast_to([P, EXPERTS, EXPERTS]),
                                                limits[:, :].unsqueeze(1).broadcast_to([P, EXPERTS, EXPERTS]), ALU.is_gt))
                chained(nc.vector.tensor_reduce(steps_of, pairs8[:, :, :], AX.X, ALU.add))
                chained(nc.vector.tensor_tensor(pairs8[:, :, :], before[:, :, :],
                                                steps_of.unsqueeze(1).broadcast_to([P, EXPERTS, EXPERTS]), ALU.mult))
                chained(nc.vector.tensor_reduce(first_step, pairs8[:, :, :], AX.X, ALU.add))
                chained(nc.vector.tensor_tensor(by_step[:, :, :], step_no[:, :].unsqueeze(2).broadcast_to([P, STEPS, EXPERTS]),
                                                first_step.unsqueeze(1).broadcast_to([P, STEPS, EXPERTS]), ALU.is_ge))
                chained(nc.vector.tensor_reduce(step_expert[:, :], by_step[:, :, :], AX.X, ALU.add))
                nc.vector.tensor_scalar(expert_of_step[:, :], step_expert[:, :], -1.0, None, ALU.add).then_inc(route_ready, 1)
                chained(nc.vector.tensor_tensor(slot[:, :, :], upto[a][:, :, :], in_tile, ALU.subtract))
                chained(nc.vector.tensor_tensor(slot[:, :, :], slot[:, :, :], within, ALU.add))
                chained(nc.vector.tensor_scalar(first_step, first_step, float(ST), None, ALU.mult))
                chained(nc.vector.tensor_tensor(slot[:, :, :], slot[:, :, :], first_step.unsqueeze(1).broadcast_to(by_tile),
                                                ALU.add))
                for r in range(TOPK):
                    chained(nc.vector.tensor_scalar(picked[:, :, :], rank[:, :, :], float(r), None, ALU.is_equal))
                    chained(nc.vector.tensor_tensor(upto[0][:, :, :], picked[:, :, :], slot[:, :, :], ALU.mult))
                    chained(nc.vector.tensor_reduce(top, upto[0][:, :, :], AX.X, ALU.add))
                    nc.vector.tensor_copy(route[:, :, r], top).then_inc(route_ready, 1)
                    chained(nc.vector.tensor_tensor(upto[0][:, :, :], picked[:, :, :], probs[:, :, :], ALU.mult))
                    chained(nc.vector.tensor_reduce(gate[:, r, :], upto[0][:, :, :], AX.X, ALU.add))
                chained(nc.vector.tensor_tensor(total, gate[:, 0, :], gate[:, 1, :], ALU.add))
                chained(nc.vector.reciprocal(inverse, total))
                chained(nc.vector.tensor_tensor(gate[:, :, :], gate[:, :, :], inverse.unsqueeze(1).broadcast_to([P, TOPK, TILES]),
                                                ALU.mult))
                nc.vector.tensor_copy(per_tile[:, 0, :], inverse).then_inc(route_ready, 1)

            def unit(n, c, width, turn_group=None, turn_c=None, p=None):
                rows = rows_of(c)
                if turn_group is not None:
                    split_weights(turn_group, turn_c, 0)
                dve.wait_ge(silu_ready, n + 1)
                dve.wait_ge(v_done, n + 1)
                if positive(n):
                    dve.wait_ge(h_lo_ready, n)
                nc.vector.tensor_tensor(hidden[0:rows, 0:width], silu_u[0:rows, 0:width], v_ps[0:rows, 0:width], ALU.mult
                                        ).then_inc(hidden_ready, 1)
                if turn_group is not None:
                    split_weights(turn_group, turn_c, 1)
                dve.wait_ge(h_hi_ready, n + 1)
                nc.vector.tensor_tensor(h_lo[0:rows, c % 2, 0:width], hidden[0:rows, 0:width],
                                        h_hi[0:rows, c % 2, 0:width].bitcast(F32), ALU.subtract).then_inc(h_lo_ready, 1)
                if turn_group is not None:
                    split_weights(turn_group, turn_c, 2)
                    if turn_c in X_JOB:
                        split_tokens(turn_group, turn_c // 2, p)

            def add_shared(tb):
                for i in range(4):
                    dve.wait_ge(out_done, 4 * tb + (i + 1))
                    tile = acc[:, bass.ds(4 * tb + i, 1), :]
                    nc.vector.tensor_tensor(tile, tile, out_ps[i][:, :].unsqueeze(1), ALU.add).then_inc(out_read, 1)

            dve.wait_ge(acc_written, TILES)
            dve.wait_ge(x_lo_ready, TILES)
            unit(0, 0, 512)
            unit(1, 1, 512)
            slots()
            for c in range(2, NC + 1):
                unit(c, c % NC, 512)
            add_shared(0)
            with dve.Fori(1, TB - 1) as tb:
                for c in range(1, NC + 1):
                    unit(tb * NC + c, c % NC, 512)
                add_shared(tb)
            for c in range(1, NC):
                unit((TB - 1) * NC + c, c, 512, 1, c - 1, 0)
            unit(TB * NC, 0, ST, 1, NC - 1, 0)
            add_shared(TB - 1)

            def step(k, p):
                for c in range(1, NC + 1):
                    unit(unit_no(k, c), c % NC, ST, k + 2, c - 1, 1 - p)

            step(0, 0)
            step(1, 1)
            with dve.Fori(1, (STEPS - 1) // 2) as half:
                step(2 * half, 0)
                step(2 * half + 1, 1)
            for c in range(1, NC):
                unit(unit_no(STEPS - 1, c), c, ST)

            dve.wait_ge(out_read, 4 * TB + 2 * STEPS)
            dve.wait_ge(route_ready, 5)
            for t in range(TILES):
                dve.wait_ge(chosen_in[t % 4], 16 * TOPK * (t // 4 + 1))
                for r in range(TOPK):
                    if r:
                        dve.wait_ge(chosen_added, TOPK * t + r)
                    nc.vector.scalar_tensor_tensor(out=acc[:, t, :], in0=chosen[:, t % 4, r, :],
                                                   scalar=gate[:, r, t:t + 1], in1=acc[:, t, :],
                                                   op0=ALU.mult, op1=ALU.add).then_inc(chosen_added, 1)

        @block.tensor
        def _(pe):
            pe.wait_ge(ident_ready, 1)

            def turn(dst, src, rows=P, cols=P, step=P, signal=None, count=LB):
                for k in range(count):
                    last = nc.tensor.transpose(dst[0:cols, k * step:k * step + rows], src(k), ident[0:rows, 0:rows])
                last.then_inc(signal, 1)

            def turn_x_ctx(t, p):
                pe.wait_ge(xn_ready, t + 1)
                if not (isinstance(t, int) and t < 1):
                    pe.wait_ge(qT_ready, t)
                turn(q_ps, lambda k: xn[:, p, k * P:(k + 1) * P], signal=q_turned)
                pe.wait_ge(c_reversed, t + 1)
                if not (isinstance(t, int) and t < 1):
                    pe.wait_ge(cT_ready, t)
                turn(c_ps, lambda k: c_rev[:, (LB - 1 - k) * P:(LB - k) * P], signal=c_turned)

            def convolve(g, s):
                pe.wait_ge(t_lo_ready, g + 1)
                for lb in range(LB):
                    pe.wait_ge(kv_lo_ready, g * LB + (lb + 1))
                    if not (isinstance(g, int) and g < 1):
                        pe.wait_ge(scaled_ready, (g - 1) * LB + (lb + 1))
                    for mb in range(lb + 1):
                        d = lb - mb
                        passes = split3(t_hi[:, s, d * P:(d + 1) * P], t_lo[:, s, d * P:(d + 1) * P],
                                        kv_hi[:, s, mb, :], kv_lo[:, s, mb, :])
                        for i, (stationary, moving) in enumerate(passes):
                            last = nc.tensor.matmul(conv_ps[lb][:, :], stationary, moving,
                                                    start=(mb == 0 and i == 0), stop=(mb == lb and i == 2))
                    last.then_inc(conv_done, 1)

            def turn_attn(t, p):
                pe.wait_ge(attn_ready, 2 * LB * t + 2 * LB)
                if not (isinstance(t, int) and t < 1):
                    pe.wait_ge(acc_written, t)
                turn(attn_ps, lambda k: attnT[:, p, k, :], signal=attn_turned)

            def turn_y(t):
                pe.wait_ge(yn_ready, t + 1)
                if not (isinstance(t, int) and t < 1):
                    pe.wait_ge(x_lo_ready, t)
                turn(yn_ps, lambda k: yn[:, k * P:(k + 1) * P], signal=yn_turned)

            turn_x_ctx(0, 0)

            def step(s, p):
                last = isinstance(s, int) and s == TILES - 1
                first = isinstance(s, int) and s == 0
                convolve(2 * s, 0)
                if not last:
                    turn_x_ctx(s + 1, 1 - p)
                if not first:
                    turn_attn(s - 1, 1 - p)
                convolve(2 * s + 1, 1)
                if not first:
                    turn_y(s - 1)

            step(0, 0)
            step(1, 1)
            with pe.Fori(1, TILES // 2 - 1) as half:
                step(2 * half, 0)
                step(2 * half + 1, 1)
            step(TILES - 2, 0)
            step(TILES - 1, 1)
            turn_attn(TILES - 1, 1)
            turn_y(TILES - 1)

            def bank_read(group, q):
                before_it = first_job(group) + (q - 1)
                if positive(before_it):
                    pe.wait_ge(w_lo_ready, before_it)

            def turn_weights(group, c, m):
                q = job_of(group, c, m)
                if m == 0:
                    pe.wait_ge(w_in[c % 2], 48 * (NC // 2) * group + 48 * (c // 2 + 1))
                bank_read(group, q)
                if m < 2:
                    raw = (w1_raw, w3_raw)[m]
                    turn(w_ps[q % 2], lambda k: raw[:, c % 2, k * P:(k + 1) * P], signal=w_turned)
                else:
                    turn(w_ps[q % 2], lambda k: w2_raw[:, c % 2, k, :], signal=w_turned)

            def turn_tokens(group, i, p, fills):
                q = X_JOB[1 + 2 * i]
                if i == 0:
                    pe.wait_ge(tokens_in[p], fills)
                bank_read(group, q)
                turn(w_ps[q % 2], lambda k: tokens_raw[:, p, i, k * P:(k + 1) * P], signal=w_turned)

            pe.wait_ge(x_lo_ready, TILES)
            for c in range(NC):
                for m in range(3):
                    turn_weights(0, c, m)

            pe.wait_ge(wr_in, 16)
            pe.wait_ge(w_lo_ready, JOBS)
            turn(wr_ps, lambda k: wr_rows[:, k * P:(k + 1) * P], rows=EXPERTS, step=EXPERTS, signal=wr_turned)
            pe.wait_ge(wr_lo_ready, 1)
            for tb in range(TB):
                for k in range(LB):
                    cols = slice(tb * 512, (tb + 1) * 512)
                    passes = split3(wr_hi[:, k, :], wr_lo[:, k, :], x_hi[:, k, cols], x_lo[:, k, cols])
                    for i, (stationary, moving) in enumerate(passes):
                        last = nc.tensor.matmul(banks[tb][0:EXPERTS, :], stationary, moving,
                                                start=(k == 0 and i == 0), stop=(k == LB - 1 and i == 2))
                last.then_inc(logits_done, 1)
            for t in range(TILES):
                if t % 4 == 0:
                    pe.wait_ge(logitsT_ready, t // 4 + 1)
                last = nc.tensor.transpose(router_ps[:, 128 + t * EXPERTS:128 + (t + 1) * EXPERTS],
                                           logitsT[:, t // 4, (t % 4) * P:(t % 4 + 1) * P],
                                           ident[0:EXPERTS, 0:EXPERTS])
            last.then_inc(logits_turned, 1)

            def count_picks():
                pe.wait_ge(route_steps, PICKED_STEP)
                pe.wait_ge(masks_ready, 5)
                picks = picked[:, :, :].rearrange("p t e -> p (t e)")
                nc.tensor.matmul(router_ps[:, 256:384], earlier[:, :], picks, start=True, stop=True)
                nc.tensor.matmul(router_ps[:, 384:512], ones[:, :], picks, start=True, stop=True).then_inc(counted, 1)

            def up(n, c, which, x_cols, width, w_ready):
                rows = rows_of(c)
                bank = (u_ps, v_ps)[which]
                if isinstance(w_ready, int) and not isinstance(n, int):
                    n = pe.to_reg(n)
                pe.wait_ge(w_lo_ready, w_ready)
                if positive(n):
                    pe.wait_ge((silu_ready, hidden_ready)[which], n)
                w_hi, w_lo = ((w1_hi, w1_lo), (w3_hi, w3_lo))[which]
                for k in range(LB):
                    passes = split3(w_hi[:, c, k, 0:rows], w_lo[:, c, k, 0:rows], *x_cols(k))
                    for i, (stationary, moving) in enumerate(passes):
                        last = nc.tensor.matmul(bank[0:rows, 0:width], stationary, moving,
                                                start=(k == 0 and i == 0), stop=(k == LB - 1 and i == 2))
                last.then_inc((u_done, v_done)[which], 1)

            def down(n, c, w_ready, out_banks, read):
                rows = rows_of(c)
                pe.wait_ge(h_lo_ready, n + 1)
                pe.wait_ge(w_lo_ready, w_ready)
                for i, bank in enumerate(out_banks):
                    if c == 0 and positive(read(i)):
                        pe.wait_ge(out_read, read(i))
                    mine = slice(i * P, (i + 1) * P)
                    passes = split3(h_hi[0:rows, c % 2, mine], h_lo[0:rows, c % 2, mine],
                                    w2_hi[0:rows, c, :], w2_lo[0:rows, c, :])
                    for j, (stationary, moving) in enumerate(passes):
                        last = nc.tensor.matmul(bank[:, :], stationary, moving,
                                                start=(c == 0 and j == 0), stop=(c == NC - 1 and j == 2))
                    if c == NC - 1:
                        last.then_inc(out_done, 1)

            def shared_up(n, tb, c, which):
                cols = bass.ds(tb * 512, 512)
                up(n, c, which, lambda k: (x_hi[:, k, cols], x_lo[:, k, cols]), 512, job_of(0, c, which) + 1)

            def shared_down(n, tb, c):
                down(n, c, job_of(0, c, 2) + 1, out_ps, lambda i: 4 * tb + (i - 3))

            def step_up(k, c, which, p):
                group = k + 1
                ready = X_JOB[3] + 1 if c == 0 else job_of(group, c, which) + 1
                up(unit_no(k, c), c, which, lambda b: (step_hi[p][:, b, :], step_lo[p][:, b, :]), ST,
                   first_job(group) + ready)

            def step_down(k, c, p):
                group = k + 1
                first = isinstance(k, int) and k == 0
                down(unit_no(k, c), c, first_job(group) + (job_of(group, c, 2) + 1), out_ps[2 * p:2 * p + 2],
                     lambda i: 4 * TB if first else 4 * TB + 2 * k - 2)

            shared_up(0, 0, 0, 0)
            shared_up(0, 0, 0, 1)

            def shared_block(tb, counting=False):
                for c in range(1, NC + 1):
                    for which in range(2):
                        shared_up(tb * NC + c, tb if c < NC else tb + 1, c % NC, which)
                    shared_down(tb * NC + (c - 1), tb, c - 1)
                    if counting and c == 1:
                        count_picks()

            shared_block(0, counting=True)
            with pe.Fori(1, TB - 1) as tb:
                shared_block(tb)
            tb = TB - 1
            for c in range(1, NC + 1):
                for which in range(2):
                    if c < NC:
                        shared_up(tb * NC + c, tb, c, which)
                    else:
                        step_up(0, 0, which, 0)
                    turn_weights(1, c - 1, which)
                shared_down(tb * NC + (c - 1), tb, c - 1)
                turn_weights(1, c - 1, 2)
                if c - 1 in X_JOB:
                    turn_tokens(1, (c - 1) // 2, 0, 16 * (ST // P))

            def step(k, p, fills):
                for c in range(1, NC + 1):
                    for which in range(2):
                        if c < NC:
                            step_up(k, c, which, p)
                        else:
                            step_up(k + 1, 0, which, 1 - p)
                        turn_weights(k + 2, c - 1, which)
                    step_down(k, c - 1, p)
                    turn_weights(k + 2, c - 1, 2)
                    if c - 1 in X_JOB:
                        turn_tokens(k + 2, (c - 1) // 2, 1 - p, fills)

            step(0, 0, 16 * (ST // P))
            step(1, 1, 2 * 16 * (ST // P))
            with pe.Fori(1, (STEPS - 1) // 2) as half:
                step(2 * half, 0, half * (16 * (ST // P)) + 16 * (ST // P))
                step(2 * half + 1, 1, half * (16 * (ST // P)) + 2 * 16 * (ST // P))
            k = STEPS - 1
            for c in range(1, NC):
                for which in range(2):
                    step_up(k, c, which, 0)
                step_down(k, c - 1, 0)
            step_down(k, NC - 1, 0)


_INS = ["x", "ctx_2048", "L0_xattn_ssm_kernel", "L0_xattn_D", "L0_ffn_sw1", "L0_ffn_sw2", "L0_ffn_sw3",
        "L0_ffn_ew1", "L0_ffn_ew2", "L0_ffn_ew3", "L0_ffn_wr"]


def kernel(**inputs):
    import numpy as _np
    import concourse.bacc as _bacc
    from concourse import mybir as _mybir
    from concourse.bass_utils import run_bass_kernel_spmd as _run

    nc = _bacc.Bacc("TRN2", target_bir_lowering=False, num_devices=1)
    arrays, args = {}, []
    for name in _INS:
        a = _np.ascontiguousarray(inputs[name])
        arrays[f"in_{name}_dram"] = a
        args.append(nc.dram_tensor(f"in_{name}_dram", a.shape, _mybir.dt.from_np(a.dtype), kind="ExternalInput").ap())
    out = nc.dram_tensor("out_0_dram", (BATCH, CH, L), _mybir.dt.float32, kind="ExternalOutput").ap()
    build(nc, *args, out)
    r = _run(nc, [arrays], core_ids=[0])
    return r.results[0]["out_0_dram"]
```

```python
from contextlib import ExitStack

import concourse.bass as bass
from concourse import mybir

F32 = mybir.dt.float32
F32R = mybir.dt.float32r
I32 = mybir.dt.int32
ALU = mybir.AluOpType
ACT = mybir.ActivationFunctionType
AX = mybir.AxisListType

P = 128
BATCH, CH, L = 8, 256, 512
HD = 8
HEADS = CH // HD
LB = L // P
TOK = BATCH * CH
TILES = TOK // P
HT = BATCH * HD
HH = HD // 2
OWN = BATCH * 2 * HH * HH
PAIRS = OWN + BATCH * HH * HH
EXPERTS = 8
HID = L * 4 // 3
NC = -(-HID // P)
TB = TOK // 512
TOPK = 2
ST = 256
STEPS = (TOK * TOPK + EXPERTS * (ST - 1)) // ST
SLOTS = STEPS * ST
BLOCKS = 3 * NC
PARTS = BLOCKS - 1
HC = NC // 2
TURNED = EXPERTS * NC
KROW = P + L
EPS = 1e-5


def part_no(c, m):
    return 3 * c + m - (c == NC - 1 and m > 0)


def positive(value):
    return not isinstance(value, int) or value > 0


def rows_of(c):
    return min(P, HID - c * P)


W1_AT = 64
PICKED_STEP = 12
MIN_STEPS = TOK * TOPK // ST
TOKENS_AFTER = (1, 3)


def build(nc, x, ctx_in, ssm_kernel, d_skip, sw1, sw2, sw3, ew1, ew2, ew3, wr, out):
    kpad = nc.dram_tensor("kpad", (HEADS, KROW), F32, kind="Internal").ap()
    yn_dram = nc.dram_tensor("yn_rows", (TOK, L), F32, kind="Internal").ap()
    slot_entries = nc.dram_tensor("slot_entries", (SLOTS, 2), F32, kind="Internal").ap()
    turned_dram = nc.dram_tensor("turned_weights", (TURNED, P, 3 * L), F32, kind="Internal").ap()
    result_dram = nc.dram_tensor("result_by_slot", (SLOTS, L), F32, kind="Internal").ap()

    base = 16512
    place = {"at": base}

    def sb(name, shape, dt=F32, at=None):
        size = 4
        for n in shape[1:]:
            size *= n
        if at is None:
            at = place["at"]
            place["at"] = at + (size + 31) // 32 * 32
        return nc.alloc_sbuf_tensor_at(name, shape, dt, offset=at)

    acc = sb("acc", [P, TILES, L])
    x_hi = sb("x_hi", [P, LB, TOK], F32R)
    x_lo = sb("x_lo", [P, LB, TOK], F32R)
    stage = place["at"]
    w1_hi = sb("w1_hi", [P, NC, LB, P], F32R)
    w1_lo = sb("w1_lo", [P, NC, LB, P], F32R)
    w3_hi = sb("w3_hi", [P, NC, LB, P], F32R)
    w3_lo = sb("w3_lo", [P, NC, LB, P], F32R)
    w2_hi = sb("w2_hi", [P, NC, L], F32R)
    w2_lo = sb("w2_lo", [P, NC, L], F32R)
    h_hi = sb("h_hi", [P, 2, 512], F32R)
    h_lo = sb("h_lo", [P, 2, 512], F32R)
    silu_u = sb("silu_u", [P, 512])
    hidden = sb("hidden", [P, 512])
    stage_end = place["at"]
    w_raw = sb("w_raw", [P, 2, 3 * L])
    router_area = place["at"]
    tokens_raw = sb("tokens_raw", [P, 2, ST // P, L])
    router_end = place["at"]
    x_hi_at = stage - 2 * LB * TOK * 4
    row_bytes = TOK * 4
    step_hi = [sb(f"step_hi{i}", [P, LB, ST], F32R, at=x_hi_at + 2 * i * row_bytes) for i in range(2)]
    step_lo = [sb(f"step_lo{i}", [P, LB, ST], F32R, at=x_hi_at + (2 * i + 1) * row_bytes) for i in range(2)]
    x_lo_at = x_hi_at + LB * TOK * 4
    result = sb("result", [P, 2, ST // P, L], at=x_lo_at)
    ident = sb("ident", [P, P])
    minus_half = sb("minus_half", [P, 1])
    stats = sb("stats", [P, 2, 6])
    moments = sb("moments", [P, 2, 2])
    var_eps = sb("var_eps", [P, 2])
    minus_mean = sb("minus_mean", [P, 2])
    rstd = sb("rstd", [P, 2])
    shift = sb("shift", [P, 2])
    wr_hi = sb("wr_hi", [P, LB, EXPERTS], F32R)
    wr_lo = sb("wr_lo", [P, LB, EXPERTS], F32R)
    logits = sb("logits", [P, TILES, EXPERTS])
    probs = sb("probs", [P, TILES, EXPERTS])
    rank = sb("rank", [P, TILES, EXPERTS])
    wr_rows_at = place["at"]
    picked = sb("picked", [P, TILES, EXPERTS])
    slot = sb("slot", [P, TILES, EXPERTS])
    upto = [sb(f"upto{i}", [P, TILES, EXPERTS]) for i in range(2)]
    wr_rows = sb("wr_rows", [EXPERTS, L], at=wr_rows_at)
    per_tile = sb("per_tile", [P, 3, TILES])
    gate = sb("gate", [P, TOPK, TILES])
    route = sb("route", [P, TILES, TOPK], I32)
    entry = sb("entry", [P, TILES, TOPK, 2])
    route_now = sb("route_now", [P, TOPK], I32)
    entry_now = sb("entry_now", [P, TOPK, 2])
    entries = sb("entries", [P, SLOTS // P, 2])
    stores_used = sb("stores_used", [P, 2], I32)
    ids_now = sb("ids_now", [P, 2, ST // P], I32)
    expert_of_step = sb("expert_of_step", [P, STEPS], I32)
    table_area = place["at"]
    table_end = 229368
    place["at"] = stage
    c_raw = sb("c_raw", [P, 2, L])
    c_rev = sb("c_rev", [P, L])
    xn = sb("xn", [P, 2, L])
    yn = sb("yn", [P, L])
    qT = sb("qT", [P, 2, LB, P])
    cT = sb("cT", [P, 2, LB, P])
    t_raw = sb("t_raw", [P, 2, L])
    t_hi = sb("t_hi", [P, 2, L], F32R)
    t_lo = sb("t_lo", [P, 2, L], F32R)
    kv = sb("kv", [P, LB, PAIRS])
    kv_hi = sb("kv_hi", [P, 2, LB, PAIRS], F32R)
    kv_lo = sb("kv_lo", [P, 2, LB, PAIRS], F32R)
    scaled = sb("scaled", [P, 2, HT * HD])
    attnT = sb("attnT", [P, 2, LB, P])
    place["at"] = max(place["at"], stage_end - 4 * L * 2)
    turned = sb("turned", [P, 2, 3 * L])
    w1_nat = sb("w1_nat", [P, 2, L])
    w3_nat = sb("w3_nat", [P, 2, L])
    w2_nat = sb("w2_nat", [P, 2, LB, P])
    assert place["at"] <= router_end, (place["at"], router_end)
    kern_area = x_lo_at + LB * TOK * 4 - 4096
    krows = sb("krows", [HEADS, KROW], at=kern_area)
    d_col = sb("d_col", [HEADS, 1], at=kern_area + KROW * 4)
    zero_entries = sb("zero_entries", [P, SLOTS // P * 2], at=kern_area + KROW * 4 + 32)
    place["at"] = router_area
    logitsT = sb("logitsT", [EXPERTS, TB, 512])
    place["at"] = router_area
    larger = sb("larger", [P, TILES, EXPERTS, EXPERTS])
    equal = sb("equal", [P, TILES, EXPERTS, EXPERTS])
    assert place["at"] <= router_end
    place["at"] = table_area
    before = sb("before", [P, EXPERTS, EXPERTS])
    earlier = sb("earlier", [P, P])
    ones = sb("ones", [P, P])
    limits = sb("limits", [P, TOK // ST])
    step_no = sb("step_no", [P, STEPS])
    per_expert = sb("per_expert", [P, 2, EXPERTS])
    pairs8 = sb("pairs8", [P, EXPERTS, EXPERTS])
    assert place["at"] <= table_end, (place["at"], table_end)
    place["at"] = router_area
    by_step = sb("by_step", [P, STEPS, EXPERTS])
    step_expert = sb("step_expert", [P, STEPS])
    is_used = sb("is_used", [P, 2 * (STEPS // 2 + 1)])
    used = sb("used", [P, 2])

    with ExitStack() as stack:
        def sem(name):
            return stack.enter_context(nc.semaphore(name))

        banks = [stack.enter_context(nc.psum_tensor(f"bank{i}", [P, 512], F32)) for i in range(8)]
        conv_ps = banks[0:4]
        qc_ps, y_ps, turn_ps = banks[4], banks[6], (banks[5], banks[7])
        out_ps, u_ps, v_ps, w_ps = banks[0:4], banks[4], banks[5], banks[6:8]
        wr_ps, router_ps = banks[4], banks[7]
        shared_ps = (banks[5], banks[7], banks[4], banks[6])

        zeroed = sem("zeroed"); ident_ready = sem("ident_ready"); kern_in = sem("kern_in")
        kern_skip = sem("kern_skip"); kpad_written = sem("kpad_written")
        x_in = [sem(f"x_in{i}") for i in range(2)]
        c_in = [sem(f"c_in{i}") for i in range(2)]
        t_in = [sem(f"t_in{i}") for i in range(2)]
        ln_steps = sem("ln_steps"); rstd_ready = sem("rstd_ready"); shift_ready = sem("shift_ready")
        c_reversed = sem("c_reversed"); xn_ready = sem("xn_ready")
        q_turned = sem("q_turned"); c_turned = sem("c_turned")
        qT_ready = sem("qT_ready"); cT_ready = sem("cT_ready")
        t_hi_ready = sem("t_hi_ready"); t_lo_ready = sem("t_lo_ready")
        kv_ready = sem("kv_ready"); kv_hi_ready = sem("kv_hi_ready"); kv_lo_even = sem("kv_lo_even")
        kv_lo_odd = sem("kv_lo_odd")
        conv_done = sem("conv_done"); scaled_ready = sem("scaled_ready"); attn_ready = sem("attn_ready")
        attn_turned = sem("attn_turned"); acc_written = sem("acc_written"); yn_ready = sem("yn_ready")
        yn_turned = sem("yn_turned"); x_hi_ready = sem("x_hi_ready"); x_lo_ready = sem("x_lo_ready")
        yn_stored = sem("yn_stored")
        wr_in = sem("wr_in"); wr_turned = sem("wr_turned"); wr_hi_ready = sem("wr_hi_ready")
        wr_lo_ready = sem("wr_lo_ready"); logits_done = sem("logits_done")
        logitsT_ready = sem("logitsT_ready"); logits_turned = sem("logits_turned")
        masks_filled = sem("masks_filled"); masks_ready = sem("masks_ready")
        route_steps = sem("route_steps"); exp_ready = sem("exp_ready"); counted = sem("counted")
        zeros_ready = sem("zeros_ready"); entries_cleared = sem("entries_cleared")
        route_ready = sem("route_ready"); route_copied = sem("route_copied")
        entries_written = sem("entries_written"); entries_in = sem("entries_in"); ids_copied = sem("ids_copied")
        w_in = [sem(f"w_in{i}") for i in range(2)]
        tokens_in = [sem(f"tokens_in{i}") for i in range(2)]
        nat_in = [sem(f"nat_in{i}") for i in range(2)]
        turned_copied = sem("turned_copied")
        turned_stored = [sem(f"turned_stored{i}") for i in range(2)]
        tokens_turned = sem("tokens_turned"); tokens_hi_ready = sem("tokens_hi_ready")
        tokens_lo_ready = sem("tokens_lo_ready")
        w_turned = sem("w_turned"); w_hi_ready = sem("w_hi_ready"); w_lo_ready = sem("w_lo_ready")
        u_done = sem("u_done"); v_done = sem("v_done"); silu_ready = sem("silu_ready")
        hidden_ready = sem("hidden_ready")
        h_hi_ready = sem("h_hi_ready"); h_lo_ready = sem("h_lo_ready")
        out_done = sem("out_done"); out_read = sem("out_read")
        result_stored = [sem(f"result_stored{i}") for i in range(2)]
        results_cleared = sem("results_cleared")
        results_added = [sem(f"results_added{i}") for i in range(4)]
        out_written = sem("out_written")

        x_heads = x.rearrange("b (t s j) l -> t s b j l", s=2, j=HD)
        c_heads = ctx_in.rearrange("b (t s j) l -> t s b j l", s=2, j=HD)
        out_heads = out.rearrange("b (t s j) l -> t s b j l", s=2, j=HD)

        def split3(hi_a, lo_a, hi_b, lo_b):
            return ((hi_a, hi_b), (hi_a, lo_b), (lo_a, hi_b))

        def unit_no(step, c):
            return TB * NC + step * NC + c

        results = result_dram.rearrange("(k i p) l -> k p i l", i=ST // P, p=P)

        def split_with(k, c):
            return (k, NC - 1) if c == 1 else (k + 1, c - 2)

        def tokens_with(k, c, p):
            return (k + 1, TOKENS_AFTER.index(c - 1), 1 - p) if c - 1 in TOKENS_AFTER else None

        def turned_parts(c):
            if c < NC - 1:
                return ((slice(0, P), slice(0, 3 * L)),)
            return ((slice(0, P), slice(0, L)), (slice(0, rows_of(c)), slice(L, 2 * L)))

        def turned_before(i, experts, c):
            return (16 * HC + 16 * i) * experts + 16 * (c // 2)

        def weight_block(c, m, src, w1, w3, w2):
            rows = rows_of(c)
            if m < 2:
                src = src.rearrange("p (k c) -> p k c", c=P)
                if c == NC - 1:
                    cols = (slice(W1_AT, W1_AT + rows), slice(0, W1_AT))[m]
                    return w1[:, c, :, cols], src[:, :, 0:(rows, W1_AT)[m]]
                return (w1, w3)[m][:, c, :, :], src
            return w2[0:rows, c, :], src[0:rows, :]

        def loaded_block(c, m, w1, w3, w2):
            if c < NC - 1:
                return weight_block(c, m, w_raw[:, c % 2, m * L:(m + 1) * L], w1, w3, w2)
            if m == 0:
                return w1[:, c, :, :], w_raw[:, c % 2, 0:L].rearrange("p (k c) -> p k c", c=P)
            return w2[0:rows_of(c), c, :], w_raw[0:rows_of(c), c % 2, L:2 * L]

        block = stack.enter_context(nc.Block())

        @block.sync
        def _(sp):
            sp.dma_start(krows[:, P:KROW], ssm_kernel).then_inc(kern_in, 16)
            sp.dma_start(d_col[:, :], d_skip.rearrange("(h o) -> h o", o=1)).then_inc(kern_in, 16)

            def load_tile(t, p):
                if not (isinstance(t, int) and t < 2):
                    used = sp.to_reg(t - 1)
                    sp.wait_ge(xn_ready, used)
                    sp.wait_ge(c_reversed, used)
                for s in range(2):
                    sp.dma_start(acc[s * HT:(s + 1) * HT, bass.ds(t, 1), :].rearrange("p o l -> p (o l)"),
                                 x_heads[bass.ds(t, 1), s, :, :, :].rearrange("o b j l -> (o b) j l")
                                 ).then_inc(x_in[p], 16)
                    sp.dma_start(c_raw[s * HT:(s + 1) * HT, p, :],
                                 c_heads[bass.ds(t, 1), s, :, :, :].rearrange("o b j l -> (o b) j l")
                                 ).then_inc(c_in[p], 16)

            def load_table(t, s):
                if not (isinstance(t, int) and t < 1):
                    used = sp.to_reg(2 * t + s - 1)
                    sp.wait_ge(t_lo_ready, used)
                sp.dma_start(t_raw[:, s, :],
                             bass.AP(kpad.tensor, t * (2 * KROW) + (s * KROW + 1), [[1, P], [1, L]])
                             ).then_inc(t_in[s], 16)

            def load_nat(q, e, c):
                w1, w3, w2 = (sw1, sw3, sw2) if e is None else (
                    w[bass.ds(e, 1), :, :].rearrange("o r c -> (o r) c") for w in (ew1, ew3, ew2))
                rows, slot_no = rows_of(c), c % 2
                if not (isinstance(q, int) and q < 2):
                    used = 3 * q - 3
                    sp.wait_ge(w_turned, used if isinstance(q, int) else sp.to_reg(used))
                for raw, w in ((w1_nat, w1), (w3_nat, w3)):
                    sp.dma_start(raw[0:rows, slot_no, :], w[c * P:c * P + rows, :]).then_inc(nat_in[slot_no], 16)
                sp.dma_start(w2_nat[:, slot_no, :, 0:rows],
                             w2[:, c * P:c * P + rows].rearrange("(d p) h -> p d h", p=P)
                             ).then_inc(nat_in[slot_no], 16)

            def store_turned(q, c):
                done = 3 * q + 3
                sp.wait_ge(turned_copied, done if isinstance(q, int) else sp.to_reg(done))
                rows = turned_dram[bass.ds(q, 1), :, :].rearrange("o p l -> (o p) l")
                for part, columns in turned_parts(c):
                    sp.dma_start(rows[part, columns], turned[part, c % 2, columns]).then_inc(turned_stored[c % 2], 16)

            def store_yn(t):
                done = t + 1 if isinstance(t, int) else sp.to_reg(t + 1)
                sp.wait_ge(yn_ready, done)
                sp.dma_start(yn_dram.rearrange("(t p) l -> t p l", p=P)[bass.ds(t, 1), :, :
                                                                       ].rearrange("o p l -> (o p) l"),
                             yn[:, :]).then_inc(yn_stored, 16)

            load_tile(0, 0)
            load_tile(1, 1)
            sp.dma_start(wr_rows[:, :], wr).then_inc(wr_in, 16)
            sp.wait_ge(kern_skip, 1)
            sp.wait_ge(zeroed, 2)
            sp.dma_start(kpad, krows[:, :]).then_inc(kpad_written, 16)
            sp.wait_ge(kpad_written, 16)
            load_table(0, 0)
            load_table(0, 1)
            load_nat(0, 0, 0)
            load_nat(1, 0, 1)
            load_table(1, 0)
            sp.wait_ge(zeros_ready, 1)
            sp.dma_start(slot_entries.rearrange("(p c) o -> p (c o)", p=P), zero_entries[:, :]
                         ).then_inc(entries_cleared, 16)

            def ahead(t, p, e):
                load = [(NC * e + HC * p + (i - 4), e - 1 if HC * p + i < 4 else e, (HC * p + i - 4) % NC)
                        for i in range(HC)]
                store = [(NC * e + HC * p + (i - 2 * HC), (HC * p + i) % NC) for i in range(HC)]
                tiles = not (isinstance(t, int) and t >= TILES)

                def load_chunk_ahead(i):
                    q, expert, c = load[i]
                    shared = isinstance(q, int) and q >= TURNED
                    load_nat(q, None if shared else expert, c)

                if tiles:
                    load_tile(t, p)
                load_chunk_ahead(0)
                store_turned(*store[0])
                if not (isinstance(t, int) and t > TILES):
                    load_table(t - 1, 1)
                load_chunk_ahead(1)
                store_turned(*store[1])
                if tiles:
                    load_table(t, 0)
                load_chunk_ahead(2)
                if not (isinstance(t, int) and t < 3):
                    store_yn(t - 3)
                store_turned(*store[2])

            ahead(2, 0, 1)
            ahead(3, 1, 1)
            with sp.Fori(2, TILES // 2) as half:
                for p in range(2):
                    ahead(2 * half + p, p, half)
            ahead(TILES, 0, EXPERTS)
            ahead(TILES + 1, 1, EXPERTS)
            store_yn(TILES - 1)
            for c in range(2, NC):
                load_nat(TURNED + c, None, c)

            sp.wait_ge(zeros_ready, 2)
            for k in range(MIN_STEPS, STEPS):
                sp.dma_start(results[k, :, :, :].rearrange("p i l -> p i l"),
                             w_raw[:, 0, 0:ST // P * L].rearrange("p (i l) -> p i l", l=L)
                             ).then_inc(results_cleared, 16)

            sp.wait_ge(entries_written, 16 * TOPK * TILES)
            sp.dma_start(entries[:, :, :], slot_entries.rearrange("(c p) o -> p c o", p=P),
                         allow_slow_non_contiguous=True).then_inc(entries_in, 16)

            def store_result(step, slot_no):
                copied = 4 * TB + 2 * step + 2
                sp.wait_ge(out_read, copied if isinstance(copied, int) else sp.to_reg(copied))
                sp.dma_start(results[bass.ds(step, 1), :, :, :].rearrange("o p i l -> (o p) i l"),
                             result[:, slot_no, :, :]).then_inc(result_stored[slot_no], 16)

            def load_step(step, back):
                expert = sp.value_load(expert_of_step[0:1, bass.ds(step, 1)], min_val=0, max_val=EXPERTS - 1)
                for c in range(NC):
                    split = PARTS * step + (BLOCKS + (3 * c - 3 if c >= 2 else 2 * c - 2))
                    sp.wait_ge(w_lo_ready, split if isinstance(step, int) else sp.to_reg(split))
                    rows = turned_dram.rearrange("(e c) p l -> e c p l", c=NC)[bass.ds(expert, 1), c, :, :
                                                                               ].rearrange("o p l -> (o p) l")
                    for part, columns in turned_parts(c):
                        sp.dma_start(w_raw[part, c % 2, columns], rows[part, columns]).then_inc(w_in[c % 2], 16)
                    if c == 2 and back is not None:
                        store_result(step - 2, back)

            sp.wait_ge(results_cleared, 16 * (STEPS - MIN_STEPS))
            load_step(0, None)
            load_step(1, None)
            load_step(2, 0)
            with sp.Fori(1, (STEPS - 1) // 2) as half:
                load_step(2 * half + 1, 1)
                load_step(2 * half + 2, 0)

            with sp.Fori(0, TILES // 4) as quarter:
                added = sp.to_reg(quarter * (16 * TOPK) + 16 * TOPK)
                for i in range(4):
                    sp.wait_ge(results_added[i], added)
                    t = 4 * quarter + i
                    for s in range(2):
                        sp.dma_start(out_heads[bass.ds(t, 1), s, :, :, :].rearrange("o b j l -> (o b) j l"),
                                     acc[s * HT:(s + 1) * HT, bass.ds(t, 1), :].rearrange("p o l -> p (o l)")
                                     ).then_inc(out_written, 16)
            for i in range(2):
                sp.wait_ge(result_stored[i], 16 * ((STEPS + 1 - i) // 2))
            sp.wait_ge(out_written, 16 * 2 * TILES)

        @block.gpsimd
        def _(pool):
            nc.gpsimd.memset(krows[:, 0:P], 0.0).then_inc(zeroed, 1)
            nc.gpsimd.memset(minus_half[:, :], -0.5).then_inc(zeroed, 1)
            nc.gpsimd.memset(ident[:, :], 0.0).then_inc(zeroed, 1)
            nc.gpsimd.memset(zero_entries[:, :], 0.0).then_inc(zeros_ready, 1)
            pool.wait_ge(zeroed, 3)
            nc.gpsimd.affine_select(out=ident[:, :], in_=ident[:, :], compare_op=ALU.not_equal, fill=1.0,
                                    base=0, pattern=[[-1, P]], channel_multiplier=1).then_inc(ident_ready, 1)

            nc.gpsimd.memset(before[:, :, :], 1.0).then_inc(masks_filled, 1)
            nc.gpsimd.memset(earlier[:, :], 1.0).then_inc(masks_filled, 1)
            nc.gpsimd.memset(ones[:, :], 1.0).then_inc(masks_ready, 1)
            pool.wait_ge(masks_filled, 2)
            nc.gpsimd.affine_select(out=before[:, :, :], in_=before[:, :, :], compare_op=ALU.is_gt, fill=0.0,
                                    base=0, pattern=[[1, EXPERTS], [-1, EXPERTS]], channel_multiplier=0
                                    ).then_inc(masks_ready, 1)
            nc.gpsimd.affine_select(out=earlier[:, :], in_=earlier[:, :], compare_op=ALU.is_gt, fill=0.0,
                                    base=0, pattern=[[1, P]], channel_multiplier=-1).then_inc(masks_ready, 1)
            nc.gpsimd.iota(limits[:, :], [[ST, TOK // ST]], base=0, channel_multiplier=0,
                           allow_small_or_imprecise_dtypes=True).then_inc(masks_ready, 1)
            nc.gpsimd.iota(step_no[:, :], [[1, STEPS]], base=0, channel_multiplier=0,
                           allow_small_or_imprecise_dtypes=True).then_inc(masks_ready, 1)
            nc.gpsimd.iota(entry[:, :, :, 0:1], [[P, TILES], [0, TOPK], [1, 1]], base=0, channel_multiplier=1,
                           allow_small_or_imprecise_dtypes=True).then_inc(route_ready, 1)

            def ln_tail(n, k):
                pool.wait_ge(ln_steps, 4 * n)
                nc.gpsimd.tensor_tensor(rstd[:, k:k + 1], var_eps[:, k:k + 1], minus_half[:, :], ALU.pow
                                        ).then_inc(rstd_ready, 1)
                pool.wait_ge(rstd_ready, n)
                nc.gpsimd.tensor_tensor(shift[:, k:k + 1], minus_mean[:, k:k + 1], rstd[:, k:k + 1], ALU.mult
                                        ).then_inc(shift_ready, 1)

            def split_table(g, s):
                pool.wait_ge(t_hi_ready, g + 1)
                if not (isinstance(g, int) and g < 2):
                    pool.wait_ge(conv_done, LB * (g - 1))
                nc.gpsimd.tensor_tensor(t_lo[:, s, :], t_raw[:, s, :], t_hi[:, s, :].bitcast(F32),
                                        ALU.subtract).then_inc(t_lo_ready, 1)

            def product(g, s, p, k, tile):
                if k == 0:
                    pool.wait_ge(cT_ready, tile + 1)
                if not (isinstance(g, int) and g < 1):
                    pool.wait_ge((kv_lo_even, kv_lo_odd)[k % 2], 2 * g + (k // 2 - 1))
                halves = cT[:, p, k, s * HT:(s + 1) * HT].rearrange("p (n j) -> p n j", j=HH)
                nc.gpsimd.tensor_tensor(kv[:, k, 0:OWN].rearrange("p (n j i) -> p n j i", j=HH, i=HH),
                                        halves.unsqueeze(3).broadcast_to([P, 2 * BATCH, HH, HH]),
                                        halves.unsqueeze(2).broadcast_to([P, 2 * BATCH, HH, HH]), ALU.mult)
                first, second = halves[:, 0::2, :], halves[:, 1::2, :]
                nc.gpsimd.tensor_tensor(kv[:, k, OWN:PAIRS].rearrange("p (b j i) -> p b j i", j=HH, i=HH),
                                        first.unsqueeze(3).broadcast_to([P, BATCH, HH, HH]),
                                        second.unsqueeze(2).broadcast_to([P, BATCH, HH, HH]),
                                        ALU.mult).then_inc(kv_ready, 1)

            def split_odd(g, s, k):
                pool.wait_ge(kv_hi_ready, g * LB + (k + 1))
                nc.gpsimd.tensor_tensor(kv_lo[:, s, k, :], kv[:, k, :], kv_hi[:, s, k, :].bitcast(F32),
                                        ALU.subtract).then_inc(kv_lo_odd, 1)

            ln_tail(1, 0)
            for k in range(LB):
                product(0, 0, 0, k, 0)
                if k % 2:
                    split_odd(0, 0, k)
                if k == 1:
                    split_table(0, 0)

            def step(s, p):
                last = isinstance(s, int) and s == TILES - 1
                first = isinstance(s, int) and s == 0
                product(2 * s + 1, 1, p, 0, s)
                product(2 * s + 1, 1, p, 1, s)
                split_odd(2 * s + 1, 1, 1)
                product(2 * s + 1, 1, p, 2, s)
                split_table(2 * s + 1, 1)
                product(2 * s + 1, 1, p, 3, s)
                if not last:
                    ln_tail(2 if first else 2 * s + 1, 0)
                if not last:
                    product(2 * s + 2, 0, 1 - p, 0, s + 1)
                split_odd(2 * s + 1, 1, 3)
                if not last:
                    product(2 * s + 2, 0, 1 - p, 1, s + 1)
                if not first:
                    ln_tail(2 * s + 1 if last else 2 * s + 2, 1)
                if not last:
                    split_odd(2 * s + 2, 0, 1)
                    product(2 * s + 2, 0, 1 - p, 2, s + 1)
                    split_table(2 * s + 2, 0)
                    product(2 * s + 2, 0, 1 - p, 3, s + 1)
                    split_odd(2 * s + 2, 0, 3)

            step(0, 0)
            step(1, 1)
            with pool.Fori(1, TILES // 2 - 1) as half:
                step(2 * half, 0)
                step(2 * half + 1, 1)
            step(TILES - 2, 0)
            step(TILES - 1, 1)
            ln_tail(2 * TILES, 1)

            for i in range(2):
                pool.wait_ge(turned_stored[i], turned_before(i, EXPERTS, 0))
            pool.wait_ge(w_turned, 3 * (TURNED + NC))
            nc.gpsimd.memset(w_raw[:, 0, 0:ST // P * L], 0.0).then_inc(zeros_ready, 1)

            pool.wait_ge(route_ready, 6)
            pool.wait_ge(entries_cleared, 16)
            with pool.Fori(0, TILES) as t:
                nc.gpsimd.tensor_copy(route_now[:, :], route[:, bass.ds(t, 1), :].rearrange("p o r -> p (o r)")
                                      ).then_inc(route_copied, 1)
                nc.gpsimd.tensor_copy(entry_now[:, :, :], entry[:, bass.ds(t, 1), :, :].rearrange("p o r e -> p (o r) e")
                                      ).then_inc(route_copied, 1)
                copied, free = pool.to_reg(2 * t + 2), pool.to_reg(t * (16 * TOPK) + 16)
                for r in range(TOPK):
                    pool.wait_ge(route_ready, 6)
                    if r == 0:
                        pool.wait_ge(route_copied, copied)
                    else:
                        pool.wait_ge(entries_written, free)
                    pool.indirect_dma_start(slot_entries, bass.IndirectOffsetOnAxis(route_now[:, r:r + 1], 0),
                                            entry_now[:, r, :], None).then_inc(entries_written, 16)
                written = pool.to_reg(t * (16 * TOPK) + 16 * TOPK)
                pool.wait_ge(entries_written, written)

            pool.wait_ge(entries_in, 16)
            pool.wait_ge(yn_stored, 16 * TILES)
            pool.wait_ge(route_ready, 6)

            def gather_tokens(step, p, before_it):
                if not isinstance(before_it, int):
                    before_it = pool.to_reg(before_it * 16)
                    pool.wait_ge(entries_in, 16)
                    pool.wait_ge(tokens_in[p], before_it)
                elif before_it:
                    pool.wait_ge(tokens_in[p], 16 * before_it)
                nc.gpsimd.tensor_copy(ids_now[:, p, :].unsqueeze(2), entries[:, bass.ds(step * (ST // P), ST // P), 0:1]
                                      ).then_inc(ids_copied, 1)
                copied, free = step + 1, 2 * step - 2
                if not isinstance(step, int):
                    copied, free = pool.to_reg(copied), pool.to_reg(free)
                pool.wait_ge(entries_in, 16)
                pool.wait_ge(ids_copied, copied)
                if not (isinstance(step, int) and step < 2):
                    pool.wait_ge(tokens_turned, free)
                for i in range(ST // P):
                    pool.indirect_dma_start(tokens_raw[:, p, i, :], None, yn_dram,
                                            bass.IndirectOffsetOnAxis(ids_now[:, p, i:i + 1], 0)
                                            ).then_inc(tokens_in[p], 16)

            gather_tokens(0, 0, 0)
            gather_tokens(1, 1, 0)
            with pool.Fori(1, STEPS // 2) as half:
                gather_tokens(2 * half, 0, (ST // P) * half)
                gather_tokens(2 * half + 1, 1, (ST // P) * half)
            gather_tokens(STEPS - 1, 0, (ST // P) * (STEPS // 2))

            stored = [pool.value_load(stores_used[0:1, i:i + 1], min_val=16, max_val=16 * ((STEPS + 1 - i) // 2))
                      for i in range(2)]
            for i in range(2):
                pool.wait_ge(results_cleared, 16 * (STEPS - MIN_STEPS))
                pool.wait_ge(result_stored[i], stored[i])
            for quarter in range(TILES // 4):
                for r in range(TOPK):
                    for i in range(4):
                        if quarter or r:
                            pool.wait_ge(results_added[i], 16 * TOPK * quarter + 16 * r)
                        pool.indirect_dma_start(acc[:, 4 * quarter + i, :], None, result_dram,
                                                bass.IndirectOffsetOnAxis(route[:, 4 * quarter + i, r:r + 1], 0),
                                                compute_op=ALU.add).then_inc(results_added[i], 16)

        @block.scalar
        def _(act):
            def reverse_ctx(t, p, use):
                act.wait_ge(c_in[p], use)
                if not (isinstance(t, int) and t < 1):
                    act.wait_ge(c_turned, t)
                nc.scalar.activation(c_rev[:, :], c_raw[:, p, ::-1], ACT.Copy).then_inc(c_reversed, 1)

            def normalise_x(t, p, n):
                act.wait_ge(shift_ready, n)
                if not (isinstance(t, int) and t < 2):
                    act.wait_ge(q_turned, t - 1)
                nc.scalar.activation(xn[:, p:p + 1, :], acc[:, bass.ds(t, 1), :], ACT.Identity, bias=shift[:, 0:1],
                                     scale=rstd[:, 0:1]).then_inc(xn_ready, 1)

            def round_table(g, s, use):
                act.wait_ge(t_in[s], use)
                if not (isinstance(g, int) and g < 2):
                    act.wait_ge(conv_done, LB * (g - 1))
                nc.scalar.activation(t_hi[:, s, :], t_raw[:, s, :], ACT.Copy).then_inc(t_hi_ready, 1)

            def copy_turned(h, p, j):
                i, m = j // 3, j % 3
                c = HC * p + i
                n = (BLOCKS * h) + (BLOCKS // 2 * p + j)
                act.wait_ge(w_turned, n + 1)
                if m == 0 and not (isinstance(h, int) and NC * h + HC * p + i < 2):
                    act.wait_ge(turned_stored[c % 2], turned_before(c % 2, h, c))
                dst, src = turned[:, c % 2, m * L:(m + 1) * L], turn_ps[(p + j) % 2][:, :]
                if c == NC - 1 and m < 2:
                    half = (slice(W1_AT, P), slice(0, W1_AT))[m]
                    dst = turned[:, 1, 0:L].rearrange("p (k c) -> p k c", c=P)[:, :, half]
                    src = src.rearrange("p (k c) -> p k c", c=P)[:, :, 0:W1_AT]
                elif c == NC - 1:
                    dst, src = turned[0:rows_of(c), 1, L:2 * L], src[0:rows_of(c), :]
                nc.scalar.activation(dst, src, ACT.Copy).then_inc(turned_copied, 1)

            def round_product(g, s, k):
                act.wait_ge(kv_ready, g * LB + (k + 1))
                if k == 0 and not (isinstance(g, int) and g < 2):
                    act.wait_ge(conv_done, LB * (g - 1))
                nc.scalar.activation(kv_hi[:, s, k, :], kv[:, k, :], ACT.Copy).then_inc(kv_hi_ready, 1)

            def keep_q(t, p):
                act.wait_ge(q_turned, t + 1)
                if not (isinstance(t, int) and t < 2):
                    act.wait_ge(scaled_ready, 2 * LB * (t - 1))
                nc.scalar.activation(qT[:, p, :, :].rearrange("p k c -> p (k c)"), qc_ps[:, :], ACT.Copy
                                     ).then_inc(qT_ready, 1)

            def keep_c(t, p):
                act.wait_ge(c_turned, t + 1)
                if not (isinstance(t, int) and t < 2):
                    act.wait_ge(kv_ready, 2 * LB * (t - 1))
                nc.scalar.activation(cT[:, p, :, :].rearrange("p k c -> p (k c)"), qc_ps[:, :], ACT.Copy
                                     ).then_inc(cT_ready, 1)

            def normalise_y(t, n):
                act.wait_ge(shift_ready, n)
                if not (isinstance(t, int) and t < 1):
                    act.wait_ge(yn_turned, t)
                    act.wait_ge(yn_stored, 16 * t)
                nc.scalar.activation(yn[:, :].unsqueeze(1), acc[:, bass.ds(t, 1), :], ACT.Identity,
                                     bias=shift[:, 1:2], scale=rstd[:, 1:2]).then_inc(yn_ready, 1)

            def round_x(t):
                act.wait_ge(yn_turned, t + 1)
                nc.scalar.activation(x_hi[:, :, bass.ds(t * P, P)], y_ps[:, :].rearrange("p (k c) -> p k c", c=P),
                                     ACT.Copy).then_inc(x_hi_ready, 1)

            reverse_ctx(0, 0, 32)
            keep_c(0, 0)
            normalise_x(0, 0, 1)
            keep_q(0, 0)
            for k in range(LB):
                round_product(0, 0, k)
                if k == 1:
                    round_table(0, 0, 16)

            def step(s, p, nth):
                last = isinstance(s, int) and s == TILES - 1
                first = isinstance(s, int) and s == 0
                if not last:
                    reverse_ctx(s + 1, 1 - p, 32 * (nth + p) + 32)
                round_product(2 * s + 1, 1, 0)
                copy_turned(nth, p, 0)
                round_product(2 * s + 1, 1, 1)
                round_table(2 * s + 1, 1, 16 * s + 16)
                copy_turned(nth, p, 1)
                round_product(2 * s + 1, 1, 2)
                if not last:
                    keep_c(s + 1, 1 - p)
                copy_turned(nth, p, 2)
                round_product(2 * s + 1, 1, 3)
                copy_turned(nth, p, 3)
                if not last:
                    normalise_x(s + 1, 1 - p, 2 if first else 2 * s + 1)
                copy_turned(nth, p, 4)
                if not last:
                    round_product(2 * s + 2, 0, 0)
                copy_turned(nth, p, 5)
                if not last:
                    round_product(2 * s + 2, 0, 1)
                    round_table(2 * s + 2, 0, 16 * s + 32)
                    keep_q(s + 1, 1 - p)
                copy_turned(nth, p, 6)
                if not first:
                    normalise_y(s - 1, 2 * s + 1 if last else 2 * s + 2)
                if not last:
                    round_product(2 * s + 2, 0, 2)
                copy_turned(nth, p, 7)
                if not last:
                    round_product(2 * s + 2, 0, 3)
                copy_turned(nth, p, 8)
                if not first:
                    round_x(s - 1)

            step(0, 0, 0)
            step(1, 1, 0)
            with act.Fori(1, TILES // 2 - 1) as half:
                step(2 * half, 0, half)
                step(2 * half + 1, 1, half)
            step(TILES - 2, 0, TILES // 2 - 1)
            step(TILES - 1, 1, TILES // 2 - 1)
            act.wait_ge(wr_turned, 1)
            nc.scalar.activation(wr_hi[:, :, :], wr_ps[:, 0:LB * EXPERTS].rearrange("p (k e) -> p k e", e=EXPERTS),
                                 ACT.Copy).then_inc(wr_hi_ready, 1)
            normalise_y(TILES - 1, 2 * TILES)
            round_x(TILES - 1)

            for c in range(NC):
                if c == NC - 1:
                    act.wait_ge(yn_stored, 16 * TILES)
                for m in range(3):
                    n = 3 * c + m
                    act.wait_ge(w_turned, 3 * TURNED + n + 1)
                    dst, src = weight_block(c, m, shared_ps[n % 4][:, :], w1_hi, w3_hi, w2_hi)
                    nc.scalar.activation(dst, src, ACT.Copy).then_inc(w_hi_ready, 1)

            def round_weights(step, c, m):
                if m == 0:
                    act.wait_ge(w_in[c % 2], turned_before(c % 2, step, c) + 16 * len(turned_parts(c)))
                if c == NC - 1 and m == 1:
                    return
                dst, src = loaded_block(c, m, w1_hi, w3_hi, w2_hi)
                nc.scalar.activation(dst, src, ACT.Copy).then_inc(w_hi_ready, 1)

            def round_tokens(step, i, p):
                act.wait_ge(tokens_turned, 2 * step + (i + 1))
                nc.scalar.activation(step_hi[p][:, :, i * P:(i + 1) * P],
                                     w_ps[i][:, :].rearrange("p (k c) -> p k c", c=P), ACT.Copy
                                     ).then_inc(tokens_hi_ready, 1)

            for tb in range(TB):
                act.wait_ge(logits_done, tb + 1)
                nc.scalar.activation(logitsT[:, tb, :], banks[tb][0:EXPERTS, :], ACT.Copy).then_inc(logitsT_ready, 1)
            act.wait_ge(route_steps, 3)
            nc.scalar.activation(probs[:, :, :], logits[:, :, :], ACT.Exp).then_inc(exp_ready, 1)

            def unit(n, c, width, split=None, tokens=None):
                rows = rows_of(c)
                act.wait_ge(u_done, n + 1)
                if positive(n):
                    act.wait_ge(hidden_ready, n)
                u_rows = slice(W1_AT, W1_AT + rows) if c == NC - 1 else slice(0, rows)
                nc.scalar.activation(silu_u[0:rows, 0:width], u_ps[u_rows, 0:width], ACT.Silu).then_inc(silu_ready, 1)
                if split:
                    round_weights(*split, 0)
                    round_weights(*split, 1)
                act.wait_ge(hidden_ready, n + 1)
                nc.scalar.activation(h_hi[0:rows, c % 2, 0:width], hidden[0:rows, 0:width], ACT.Copy
                                     ).then_inc(h_hi_ready, 1)
                if split:
                    round_weights(*split, 2)
                if tokens:
                    round_tokens(*tokens)

            def keep_result(step, p):
                for i in range(ST // P):
                    act.wait_ge(out_done, 4 * TB + 2 * step + (i + 1))
                    if i == 0 and not (isinstance(step, int) and step < 2):
                        act.wait_ge(result_stored[p], result_fills)
                    nc.scalar.activation(result[:, p, i:i + 1, :], out_ps[2 * p + i][:, :].unsqueeze(1), ACT.Copy,
                                         scale=entries[:, bass.ds(step * (ST // P) + i, 1), 1]).then_inc(out_read, 1)

            unit(0, 0, 512)
            with act.Fori(0, TB - 1) as tb:
                for c in range(1, NC + 1):
                    unit(tb * NC + c, c % NC, 512)
            for c in range(1, NC + 1):
                unit((TB - 1) * NC + c, c % NC, 512 if c < NC else ST, split_with(-1, c) if c > 1 else None,
                     tokens_with(-1, c, 1))

            def step(k, p):
                for c in range(1, NC + 1):
                    unit(unit_no(k, c), c % NC, ST, split_with(k, c), tokens_with(k, c, p))
                keep_result(k, p)

            result_fills = 0
            act.wait_ge(out_read, 4 * TB)
            act.wait_ge(entries_in, 16)
            act.wait_ge(results_cleared, 16 * (STEPS - MIN_STEPS))
            step(0, 0)
            step(1, 1)
            with act.Fori(1, (STEPS - 1) // 2) as half:
                result_fills = half * 16
                step(2 * half, 0)
                step(2 * half + 1, 1)
            result_fills = 16 * ((STEPS - 1) // 2)

            def store_last(step, p):
                act.wait_ge(out_read, 4 * TB + 2 * step + 2)
                act.dma_start(results[step, :, :, :], result[:, p, :, :]).then_inc(result_stored[p], 16)

            store_last(STEPS - 2, 1)
            for c in range(1, NC):
                unit(unit_no(STEPS - 1, c), c, ST, split_with(STEPS - 1, c) if c == 1 else None)
            keep_result(STEPS - 1, 0)
            store_last(STEPS - 1, 0)

        @block.vector
        def _(dve):
            dve.wait_ge(kern_in, 32)
            nc.vector.tensor_tensor(krows[:, P:P + 1], krows[:, P:P + 1], d_col[:, :], ALU.add).then_inc(kern_skip, 1)

            def statistics(src, k):
                nc.vector.bn_stats(stats[:, k, :], src).then_inc(ln_steps, 1)

            def aggregate(n, k):
                stats_done = 4 * n - 3 if isinstance(n, int) else dve.to_reg(4 * n - 3)
                dve.wait_ge(kern_in, 32)
                dve.wait_ge(ln_steps, stats_done)
                nc.vector.bn_aggr(moments[:, k, :], stats[:, k, :]).then_inc(ln_steps, 1)

            def finish_moments(n, k):
                dve.wait_ge(ln_steps, 4 * n - 2)
                nc.vector.tensor_scalar(var_eps[:, k:k + 1], moments[:, k, 1:2], EPS, None, ALU.add
                                        ).then_inc(ln_steps, 1)
                nc.vector.tensor_scalar(minus_mean[:, k:k + 1], moments[:, k, 0:1], -1.0, None, ALU.mult
                                        ).then_inc(ln_steps, 1)

            def statistics_x(t, p, use):
                tile = t
                if not isinstance(t, int):
                    t, use = dve.to_reg(t), dve.to_reg(use)
                dve.wait_ge(kern_in, 32)
                dve.wait_ge(x_in[p], use)
                if not (isinstance(t, int) and t < 1):
                    dve.wait_ge(xn_ready, t)
                statistics(acc[:, bass.ds(tile, 1), :], 0)

            def split_block(g, s, k):
                if k % 2 == 0:
                    dve.wait_ge(kv_hi_ready, g * LB + (k + 1))
                    nc.vector.tensor_tensor(kv_lo[:, s, k, :], kv[:, k, :], kv_hi[:, s, k, :].bitcast(F32),
                                            ALU.subtract).then_inc(kv_lo_even, 1)

            def scale(g, s, p, k, tile):
                n = g * LB + (k + 1)
                dve.wait_ge(conv_done, n)
                if k == 0 and s == 0:
                    dve.wait_ge(qT_ready, tile + 1)
                if not (isinstance(n, int) and n <= 2):
                    dve.wait_ge(attn_ready, n - 2)
                q = qT[:, p, k, s * HT:(s + 1) * HT].rearrange("p (n i) -> p n i", i=HH)
                full = scaled[:, k % 2, :].rearrange("p (n j i) -> p n j i", j=HH, i=HD)
                across = conv_ps[k][:, OWN:PAIRS]
                nc.vector.tensor_tensor(full[:, :, :, 0:HH],
                                        conv_ps[k][:, 0:OWN].rearrange("p (n j i) -> p n j i", j=HH, i=HH),
                                        q.unsqueeze(2).broadcast_to([P, 2 * BATCH, HH, HH]), ALU.mult)
                nc.vector.tensor_tensor(full[:, 0::2, :, HH:HD],
                                        across.rearrange("p (b j i) -> p b j i", j=HH, i=HH),
                                        q[:, 1::2, :].unsqueeze(2).broadcast_to([P, BATCH, HH, HH]), ALU.mult)
                nc.vector.tensor_tensor(full[:, 1::2, :, HH:HD],
                                        across.rearrange("p (b j i) -> p b i j", j=HH, i=HH),
                                        q[:, 0::2, :].unsqueeze(2).broadcast_to([P, BATCH, HH, HH]), ALU.mult
                                        ).then_inc(scaled_ready, 1)

            def contract(g, s, p, k, tile):
                n = g * LB + (k + 1)
                if k == 0 and s == 0 and not (isinstance(tile, int) and tile < 2):
                    dve.wait_ge(attn_turned, tile - 1)
                dve.wait_ge(scaled_ready, n)
                nc.vector.tensor_reduce(attnT[:, p, k, s * HT:(s + 1) * HT],
                                        scaled[:, k % 2, :].rearrange("p (n i) -> p n i", i=HD), AX.X, ALU.add
                                        ).then_inc(attn_ready, 1)

            def add_residual(t):
                dve.wait_ge(attn_turned, t + 1)
                nc.vector.tensor_tensor(acc[:, bass.ds(t, 1), :], y_ps[:, :].unsqueeze(1),
                                        acc[:, bass.ds(t, 1), :], ALU.add).then_inc(acc_written, 1)

            def statistics_y(t):
                dve.wait_ge(kern_in, 32)
                dve.wait_ge(acc_written, t + 1)
                if not (isinstance(t, int) and t < 1):
                    dve.wait_ge(yn_ready, t)
                statistics(acc[:, bass.ds(t, 1), :], 1)

            def split_x(t):
                dve.wait_ge(x_hi_ready, t + 1)
                if isinstance(t, int) and t == 0:
                    dve.wait_ge(kpad_written, 16)
                    dve.wait_ge(entries_cleared, 16)
                nc.vector.tensor_tensor(x_lo[:, :, bass.ds(t * P, P)], y_ps[:, :].rearrange("p (k c) -> p k c", c=P),
                                        x_hi[:, :, bass.ds(t * P, P)].bitcast(F32), ALU.subtract
                                        ).then_inc(x_lo_ready, 1)

            statistics_x(0, 0, 32)
            aggregate(1, 0)
            finish_moments(1, 0)
            for k in range(LB):
                split_block(0, 0, k)

            def step(s, p, nth):
                last = isinstance(s, int) and s == TILES - 1
                first = isinstance(s, int) and s == 0
                n_x, n_y = 2 if first else 2 * s + 1, 2 * s + 1 if last else 2 * s + 2
                split_block(2 * s + 1, 1, 0)
                scale(2 * s, 0, p, 0, s)
                if not first:
                    contract(2 * s - 1, 1, 1 - p, 3, s - 1)
                if not last:
                    statistics_x(s + 1, 1 - p, 32 * (nth + p) + 32)
                scale(2 * s, 0, p, 1, s)
                if not last:
                    aggregate(n_x, 0)
                contract(2 * s, 0, p, 0, s)
                if not last:
                    finish_moments(n_x, 0)
                split_block(2 * s + 1, 1, 2)
                scale(2 * s, 0, p, 2, s)
                contract(2 * s, 0, p, 1, s)
                if not first:
                    add_residual(s - 1)
                scale(2 * s, 0, p, 3, s)
                if not first:
                    statistics_y(s - 1)
                contract(2 * s, 0, p, 2, s)
                if not first:
                    aggregate(n_y, 1)
                if not last:
                    split_block(2 * s + 2, 0, 0)
                if not first:
                    finish_moments(n_y, 1)
                for k in range(LB):
                    if k == 2 and not last:
                        split_block(2 * s + 2, 0, k)
                    scale(2 * s + 1, 1, p, k, s)
                    contract(2 * s + (1 if k else 0), 1 if k else 0, p, (k - 1) % LB, s)
                    if k == 3 and not first:
                        split_x(s - 1)

            step(0, 0, 0)
            step(1, 1, 0)
            with dve.Fori(1, TILES // 2 - 1) as half:
                step(2 * half, 0, half)
                step(2 * half + 1, 1, half)
            step(TILES - 2, 0, TILES // 2 - 1)
            step(TILES - 1, 1, TILES // 2 - 1)
            contract(2 * TILES - 1, 1, 1, 3, TILES - 1)
            add_residual(TILES - 1)
            statistics_y(TILES - 1)
            aggregate(2 * TILES, 1)
            finish_moments(2 * TILES, 1)
            dve.wait_ge(wr_hi_ready, 1)
            nc.vector.tensor_tensor(wr_lo[:, :, :], wr_ps[:, 0:LB * EXPERTS].rearrange("p (k e) -> p k e", e=EXPERTS),
                                    wr_hi[:, :, :].bitcast(F32), ALU.subtract).then_inc(wr_lo_ready, 1)
            split_x(TILES - 1)

            def low_part(c, m, src):
                hi = weight_block(c, m, src, w1_hi, w3_hi, w2_hi)[0]
                dst, src = weight_block(c, m, src, w1_lo, w3_lo, w2_lo)
                nc.vector.tensor_tensor(dst, src, hi.bitcast(F32), ALU.subtract).then_inc(w_lo_ready, 1)

            def split_weights(step, c, m):
                if c == NC - 1 and m == 1:
                    return
                dve.wait_ge(w_hi_ready, PARTS * step + (BLOCKS + part_no(c, m) + 1))
                hi = loaded_block(c, m, w1_hi, w3_hi, w2_hi)[0]
                dst, src = loaded_block(c, m, w1_lo, w3_lo, w2_lo)
                nc.vector.tensor_tensor(dst, src, hi.bitcast(F32), ALU.subtract).then_inc(w_lo_ready, 1)

            def split_tokens(step, i, p):
                dve.wait_ge(tokens_hi_ready, 2 * step + (i + 1))
                mine = slice(i * P, (i + 1) * P)
                nc.vector.tensor_tensor(step_lo[p][:, :, mine], w_ps[i][:, :].rearrange("p (k c) -> p k c", c=P),
                                        step_hi[p][:, :, mine].bitcast(F32), ALU.subtract).then_inc(tokens_lo_ready, 1)

            for c in range(NC):
                for m in range(3):
                    dve.wait_ge(w_hi_ready, 3 * c + m + 1)
                    low_part(c, m, shared_ps[(3 * c + m) % 4][:, :])

            by_tile = [P, TILES, EXPERTS]
            pairwise = [P, TILES, EXPERTS, EXPERTS]
            top, total, inverse = (per_tile[:, i, :] for i in range(3))
            done = [0]

            def chained(instruction):
                done[0] += 1
                instruction.then_inc(route_steps, 1)
                dve.wait_ge(route_steps, done[0])

            dve.wait_ge(masks_ready, 5)
            dve.wait_ge(logits_turned, 1)
            chained(nc.vector.tensor_copy(logits[:, :, :], router_ps[:, 128:256].rearrange("p (t e) -> p t e", e=EXPERTS)))
            chained(nc.vector.tensor_reduce(top, logits[:, :, :], AX.X, ALU.max))
            chained(nc.vector.tensor_tensor(logits[:, :, :], logits[:, :, :], top.unsqueeze(2).broadcast_to(by_tile),
                                            ALU.subtract))
            dve.wait_ge(exp_ready, 1)
            chained(nc.vector.tensor_reduce(total, probs[:, :, :], AX.X, ALU.add))
            chained(nc.vector.reciprocal(inverse, total))
            chained(nc.vector.tensor_tensor(probs[:, :, :], probs[:, :, :], inverse.unsqueeze(2).broadcast_to(by_tile),
                                            ALU.mult))
            other = probs[:, :, :].unsqueeze(2).broadcast_to(pairwise)
            mine = probs[:, :, :].unsqueeze(3).broadcast_to(pairwise)
            chained(nc.vector.tensor_tensor(larger[:, :, :, :], other, mine, ALU.is_gt))
            chained(nc.vector.tensor_tensor(equal[:, :, :, :], other, mine, ALU.is_equal))
            chained(nc.vector.tensor_tensor(equal[:, :, :, :], equal[:, :, :, :],
                                            before[:, :, :].unsqueeze(1).broadcast_to(pairwise), ALU.mult))
            chained(nc.vector.tensor_tensor(larger[:, :, :, :], larger[:, :, :, :], equal[:, :, :, :], ALU.add))
            chained(nc.vector.tensor_reduce(rank[:, :, :], larger[:, :, :, :], AX.X, ALU.add))
            chained(nc.vector.tensor_scalar(picked[:, :, :], rank[:, :, :], TOPK - 0.5, None, ALU.is_lt))
            picked_at = done[0]
            assert picked_at == PICKED_STEP

            def first_slots():
                dve.wait_ge(counted, 1)
                in_tile = router_ps[:, 384:512].rearrange("p (t e) -> p t e", e=EXPERTS)
                chained(nc.vector.tensor_copy(upto[0][:, :, :], in_tile))
                a = 0
                for d in (1, 2, 4, 8):
                    chained(nc.vector.tensor_copy(upto[1 - a][:, 0:d, :], upto[a][:, 0:d, :]))
                    chained(nc.vector.tensor_tensor(upto[1 - a][:, d:, :], upto[a][:, d:, :], upto[a][:, :TILES - d, :],
                                                    ALU.add))
                    a = 1 - a
                all_picks = upto[a][:, TILES - 1, :]
                steps_of, first_step = per_expert[:, 0, :], per_expert[:, 1, :]
                chained(nc.vector.tensor_tensor(pairs8[:, :, :], all_picks.unsqueeze(2).broadcast_to([P, EXPERTS, EXPERTS]),
                                                limits[:, :].unsqueeze(1).broadcast_to([P, EXPERTS, EXPERTS]), ALU.is_gt))
                chained(nc.vector.tensor_reduce(steps_of, pairs8[:, :, :], AX.X, ALU.add))
                chained(nc.vector.tensor_tensor(pairs8[:, :, :], before[:, :, :],
                                                steps_of.unsqueeze(1).broadcast_to([P, EXPERTS, EXPERTS]), ALU.mult))
                chained(nc.vector.tensor_reduce(first_step, pairs8[:, :, :], AX.X, ALU.add))
                chained(nc.vector.tensor_tensor(by_step[:, :, :], step_no[:, :].unsqueeze(2).broadcast_to([P, STEPS, EXPERTS]),
                                                first_step.unsqueeze(1).broadcast_to([P, STEPS, EXPERTS]), ALU.is_ge))
                chained(nc.vector.tensor_reduce(step_expert[:, :], by_step[:, :, :], AX.X, ALU.add))
                nc.vector.tensor_scalar(expert_of_step[:, :], step_expert[:, :], -1.0, None, ALU.add).then_inc(route_ready, 1)
                chained(nc.vector.tensor_reduce(used[:, 0:1], steps_of.unsqueeze(1), AX.X, ALU.add))
                chained(nc.vector.memset(is_used[:, STEPS:], 0.0))
                chained(nc.vector.tensor_scalar(is_used[:, 0:STEPS], step_no[:, :], used[:, 0:1], 16.0, ALU.is_lt,
                                                ALU.mult))
                chained(nc.vector.tensor_reduce(used[:, :], is_used[:, :].rearrange("p (h i) -> p i h", i=2), AX.X, ALU.add))
                nc.vector.tensor_copy(stores_used[:, :], used[:, :]).then_inc(route_ready, 1)

            def all_slots():
                a = 0
                within = router_ps[:, 256:384].rearrange("p (t e) -> p t e", e=EXPERTS)
                in_tile = router_ps[:, 384:512].rearrange("p (t e) -> p t e", e=EXPERTS)
                first_step = per_expert[:, 1, :]
                chained(nc.vector.tensor_tensor(slot[:, :, :], upto[a][:, :, :], in_tile, ALU.subtract))
                chained(nc.vector.tensor_tensor(slot[:, :, :], slot[:, :, :], within, ALU.add))
                chained(nc.vector.tensor_scalar(first_step, first_step, float(ST), None, ALU.mult))
                chained(nc.vector.tensor_tensor(slot[:, :, :], slot[:, :, :], first_step.unsqueeze(1).broadcast_to(by_tile),
                                                ALU.add))
                for r in range(TOPK):
                    chained(nc.vector.tensor_scalar(picked[:, :, :], rank[:, :, :], float(r), None, ALU.is_equal))
                    chained(nc.vector.tensor_tensor(upto[0][:, :, :], picked[:, :, :], slot[:, :, :], ALU.mult))
                    chained(nc.vector.tensor_reduce(top, upto[0][:, :, :], AX.X, ALU.add))
                    nc.vector.tensor_copy(route[:, :, r], top).then_inc(route_ready, 1)
                    chained(nc.vector.tensor_tensor(upto[0][:, :, :], picked[:, :, :], probs[:, :, :], ALU.mult))
                    chained(nc.vector.tensor_reduce(gate[:, r, :], upto[0][:, :, :], AX.X, ALU.add))
                chained(nc.vector.tensor_tensor(total, gate[:, 0, :], gate[:, 1, :], ALU.add))
                chained(nc.vector.reciprocal(inverse, total))
                nc.vector.tensor_tensor(entry[:, :, :, 1].rearrange("p t r -> p r t"), gate[:, :, :],
                                        inverse.unsqueeze(1).broadcast_to([P, TOPK, TILES]), ALU.mult
                                        ).then_inc(route_ready, 1)

            def unit(n, c, width, split=None, tokens=None):
                rows = rows_of(c)
                if split:
                    split_weights(*split, 0)
                dve.wait_ge(silu_ready, n + 1)
                if c < NC - 1:
                    dve.wait_ge(v_done, n + 1)
                if positive(n):
                    dve.wait_ge(h_lo_ready, n)
                nc.vector.tensor_tensor(hidden[0:rows, 0:width], silu_u[0:rows, 0:width],
                                        (u_ps if c == NC - 1 else v_ps)[0:rows, 0:width], ALU.mult
                                        ).then_inc(hidden_ready, 1)
                if split:
                    split_weights(*split, 1)
                dve.wait_ge(h_hi_ready, n + 1)
                nc.vector.tensor_tensor(h_lo[0:rows, c % 2, 0:width], hidden[0:rows, 0:width],
                                        h_hi[0:rows, c % 2, 0:width].bitcast(F32), ALU.subtract).then_inc(h_lo_ready, 1)
                if split:
                    split_weights(*split, 2)
                if tokens:
                    split_tokens(*tokens)

            def add_shared(tb):
                for i in range(4):
                    dve.wait_ge(out_done, 4 * tb + (i + 1))
                    tile = acc[:, bass.ds(4 * tb + i, 1), :]
                    nc.vector.tensor_tensor(tile, tile, out_ps[i][:, :].unsqueeze(1), ALU.add).then_inc(out_read, 1)

            dve.wait_ge(acc_written, TILES)
            dve.wait_ge(x_lo_ready, TILES)
            unit(0, 0, 512)
            unit(1, 1, 512)
            first_slots()
            unit(2, 2, 512)
            all_slots()
            for c in range(3, NC + 1):
                unit(c, c % NC, 512)
            add_shared(0)
            with dve.Fori(1, TB - 1) as tb:
                for c in range(1, NC + 1):
                    unit(tb * NC + c, c % NC, 512)
                add_shared(tb)
            for c in range(1, NC + 1):
                unit((TB - 1) * NC + c, c % NC, 512 if c < NC else ST, split_with(-1, c) if c > 1 else None,
                     tokens_with(-1, c, 1))
            add_shared(TB - 1)

            def step(k, p):
                for c in range(1, NC + 1):
                    unit(unit_no(k, c), c % NC, ST, split_with(k, c), tokens_with(k, c, p))

            step(0, 0)
            step(1, 1)
            with dve.Fori(1, (STEPS - 1) // 2) as half:
                step(2 * half, 0)
                step(2 * half + 1, 1)
            for c in range(1, NC):
                unit(unit_no(STEPS - 1, c), c, ST, split_with(STEPS - 1, c) if c == 1 else None)

        @block.tensor
        def _(pe):
            pe.wait_ge(ident_ready, 1)

            def turn(dst, src, rows=P, cols=P, step=P, signal=None, count=LB):
                for k in range(count):
                    last = nc.tensor.transpose(dst[0:cols, k * step:k * step + rows], src(k), ident[0:rows, 0:rows])
                last.then_inc(signal, 1)

            def turn_q(t, p):
                pe.wait_ge(xn_ready, t + 1)
                pe.wait_ge(cT_ready, t + 1)
                turn(qc_ps, lambda k: xn[:, p, k * P:(k + 1) * P], signal=q_turned)

            def turn_ctx(t):
                pe.wait_ge(c_reversed, t + 1)
                if not (isinstance(t, int) and t < 1):
                    pe.wait_ge(qT_ready, t)
                turn(qc_ps, lambda k: c_rev[:, (LB - 1 - k) * P:(LB - k) * P], signal=c_turned)

            def turn_block(h, p, j):
                i, m = j // 3, j % 3
                c = HC * p + i
                if m == 0:
                    pe.wait_ge(nat_in[c % 2], (48 * HC) * h + 48 * (c // 2 + 1))
                n = (BLOCKS * h) + (BLOCKS // 2 * p + j)
                if not (isinstance(n, int) and n < 2):
                    pe.wait_ge(turned_copied, n - 1)
                turn_weights(c, m, turn_ps[(p + j) % 2])

            def turn_weights(c, m, bank):
                if m < 2:
                    raw = (w1_nat, w3_nat)[m]
                    turn(bank, lambda k: raw[:, c % 2, k * P:(k + 1) * P], signal=w_turned)
                else:
                    turn(bank, lambda k: w2_nat[:, c % 2, k, :], signal=w_turned)

            def convolve(g, s, between):
                for lb in range(LB):
                    between(lb)
                    if lb == 0:
                        pe.wait_ge(t_lo_ready, g + 1)
                    pe.wait_ge((kv_lo_even, kv_lo_odd)[lb % 2], 2 * g + (lb // 2 + 1))
                    if not (isinstance(g, int) and g < 1):
                        pe.wait_ge(scaled_ready, (g - 1) * LB + (lb + 1))
                    for mb in range(lb + 1):
                        d = lb - mb
                        passes = split3(t_hi[:, s, d * P:(d + 1) * P], t_lo[:, s, d * P:(d + 1) * P],
                                        kv_hi[:, s, mb, :], kv_lo[:, s, mb, :])
                        if lb == 3 and mb == 2:
                            between(LB)
                        for i, (stationary, moving) in enumerate(passes):
                            last = nc.tensor.matmul(conv_ps[lb][:, 0:PAIRS], stationary, moving,
                                                    start=(mb == 0 and i == 0), stop=(mb == lb and i == 2))
                    last.then_inc(conv_done, 1)

            def turn_attn(t, p):
                pe.wait_ge(attn_ready, 2 * LB * t + 2 * LB)
                if not (isinstance(t, int) and t < 1):
                    pe.wait_ge(x_lo_ready, t)
                turn(y_ps, lambda k: attnT[:, p, k, :], signal=attn_turned)

            def turn_y(t):
                pe.wait_ge(acc_written, t + 1)
                pe.wait_ge(yn_ready, t + 1)
                turn(y_ps, lambda k: yn[:, k * P:(k + 1) * P], signal=yn_turned)

            turn_ctx(0)
            turn_q(0, 0)

            def step(s, p, h):
                last = isinstance(s, int) and s == TILES - 1
                first = isinstance(s, int) and s == 0

                def with_even_head(lb):
                    if lb == 2 and not last:
                        turn_ctx(s + 1)
                    if lb == 3 and not first:
                        turn_attn(s - 1, 1 - p)
                    turn_block(h, p, lb)

                def with_odd_head(lb):
                    if lb == LB:
                        return
                    if lb == 1 and not last:
                        turn_q(s + 1, 1 - p)
                    turn_block(h, p, LB + 1 + lb)
                    if lb == 3 and not first:
                        turn_y(s - 1)

                convolve(2 * s, 0, with_even_head)
                convolve(2 * s + 1, 1, with_odd_head)

            step(0, 0, 0)
            step(1, 1, 0)
            with pe.Fori(1, TILES // 2 - 1) as half:
                step(2 * half, 0, half)
                step(2 * half + 1, 1, half)
            step(TILES - 2, 0, TILES // 2 - 1)
            step(TILES - 1, 1, TILES // 2 - 1)

            def turn_tokens(step, i, p, fills):
                if i == 0:
                    pe.wait_ge(tokens_in[p], fills)
                if positive(2 * step + (i - 1)):
                    pe.wait_ge(tokens_lo_ready, 2 * step + (i - 1))
                turn(w_ps[i], lambda k: tokens_raw[:, p, i, k * P:(k + 1) * P], signal=tokens_turned)

            def turn_shared(n):
                c, m = n // 3, n % 3
                if m == 0:
                    pe.wait_ge(nat_in[c % 2], 48 * (TURNED // 2 + c // 2 + 1))
                if n >= 4:
                    pe.wait_ge(w_lo_ready, n - 3)
                turn_weights(c, m, shared_ps[n % 4])

            def logits_of(tb):
                pe.wait_ge(x_lo_ready, 4 * tb + 4)
                for k in range(LB):
                    cols = slice(tb * 512, (tb + 1) * 512)
                    passes = split3(wr_hi[:, k, :], wr_lo[:, k, :], x_hi[:, k, cols], x_lo[:, k, cols])
                    for i, (stationary, moving) in enumerate(passes):
                        last = nc.tensor.matmul(banks[tb][0:EXPERTS, :], stationary, moving,
                                                start=(k == 0 and i == 0), stop=(k == LB - 1 and i == 2))
                last.then_inc(logits_done, 1)

            pe.wait_ge(wr_in, 16)
            pe.wait_ge(qT_ready, TILES)
            turn(wr_ps, lambda k: wr_rows[:, k * P:(k + 1) * P], rows=EXPERTS, step=EXPERTS, signal=wr_turned)
            turn_attn(TILES - 1, 1)
            pe.wait_ge(turned_copied, 3 * TURNED)
            turn_shared(0)
            turn_shared(1)
            pe.wait_ge(wr_lo_ready, 1)
            pe.wait_ge(scaled_ready, 2 * LB * TILES)
            logits_of(0)
            turn_shared(2)
            turn_y(TILES - 1)
            logits_of(1)
            logits_of(2)
            pe.wait_ge(x_lo_ready, TILES)
            for n in range(3, 9):
                turn_shared(n)
            logits_of(3)
            for n in range(9, BLOCKS):
                turn_shared(n)
            pe.wait_ge(w_lo_ready, BLOCKS)

            for t in range(TILES):
                if t % 4 == 0:
                    pe.wait_ge(logitsT_ready, t // 4 + 1)
                last = nc.tensor.transpose(router_ps[:, 128 + t * EXPERTS:128 + (t + 1) * EXPERTS],
                                           logitsT[:, t // 4, (t % 4) * P:(t % 4 + 1) * P],
                                           ident[0:EXPERTS, 0:EXPERTS])
            last.then_inc(logits_turned, 1)

            def count_picks():
                pe.wait_ge(route_steps, PICKED_STEP)
                pe.wait_ge(masks_ready, 5)
                picks = picked[:, :, :].rearrange("p t e -> p (t e)")
                nc.tensor.matmul(router_ps[:, 256:384], earlier[:, :], picks, start=True, stop=True)
                nc.tensor.matmul(router_ps[:, 384:512], ones[:, :], picks, start=True, stop=True).then_inc(counted, 1)

            def up(n, c, which, x_cols, width, w_ready):
                rows = rows_of(c)
                if c == NC - 1:
                    if which:
                        return
                    rows = W1_AT + rows
                bank = (u_ps, v_ps)[which]
                read = n - 1 if which and c == 0 else n
                if isinstance(w_ready, int) and not isinstance(read, int):
                    read = pe.to_reg(read)
                pe.wait_ge(w_lo_ready, w_ready)
                if positive(read):
                    pe.wait_ge((hidden_ready if which or c == 0 else silu_ready), read)
                w_hi, w_lo = ((w1_hi, w1_lo), (w3_hi, w3_lo))[which]
                for k in range(LB):
                    passes = split3(w_hi[:, c, k, 0:rows], w_lo[:, c, k, 0:rows], *x_cols(k))
                    for i, (stationary, moving) in enumerate(passes):
                        last = nc.tensor.matmul(bank[0:rows, 0:width], stationary, moving,
                                                start=(k == 0 and i == 0), stop=(k == LB - 1 and i == 2))
                        if c == NC - 1 and k == LB - 1 and i == 1:
                            last.then_inc(v_done, 1)
                last.then_inc((u_done, v_done)[which], 1)

            def down(n, c, w_ready, out_banks, read):
                rows = rows_of(c)
                pe.wait_ge(h_lo_ready, n + 1)
                pe.wait_ge(w_lo_ready, w_ready)
                for i, bank in enumerate(out_banks):
                    if c == 0 and positive(read(i)):
                        pe.wait_ge(out_read, read(i))
                    mine = slice(i * P, (i + 1) * P)
                    passes = split3(h_hi[0:rows, c % 2, mine], h_lo[0:rows, c % 2, mine],
                                    w2_hi[0:rows, c, :], w2_lo[0:rows, c, :])
                    for j, (stationary, moving) in enumerate(passes):
                        last = nc.tensor.matmul(bank[:, :], stationary, moving,
                                                start=(c == 0 and j == 0), stop=(c == NC - 1 and j == 2))
                    if c == NC - 1:
                        last.then_inc(out_done, 1)

            def shared_up(n, tb, c, which):
                cols = bass.ds(tb * 512, 512)
                up(n, c, which, lambda k: (x_hi[:, k, cols], x_lo[:, k, cols]), 512, 3 * c + (1 if c == NC - 1 else which) + 1)

            def shared_down(n, tb, c):
                down(n, c, 3 * c + 3, out_ps, lambda i: 4 * tb + (i - 3))

            def step_up(k, c, which, p):
                if c == 0 and which == order(0)[0]:
                    pe.wait_ge(tokens_lo_ready, 2 * k + 2)
                up(unit_no(k, c), c, which, lambda b: (step_hi[p][:, b, :], step_lo[p][:, b, :]), ST,
                   PARTS * k + (BLOCKS + part_no(c, which) + 1))

            def step_down(k, c, p):
                first = isinstance(k, int) and k == 0
                down(unit_no(k, c), c, PARTS * k + (BLOCKS + part_no(c, 2) + 1), out_ps[2 * p:2 * p + 2],
                     lambda i: 4 * TB if first else 4 * TB + 2 * k - 2)

            def order(c):
                return (1, 0) if c % NC == 0 else (0, 1)

            shared_up(0, 0, 0, 0)
            shared_up(0, 0, 0, 1)

            def shared_block(tb, counting=False):
                for c in range(1, NC + 1):
                    for which in order(c):
                        shared_up(tb * NC + c, tb if c < NC else tb + 1, c % NC, which)
                    shared_down(tb * NC + (c - 1), tb, c - 1)
                    if counting and c == 1:
                        count_picks()

            shared_block(0, counting=True)
            with pe.Fori(1, TB - 1) as tb:
                shared_block(tb)
            tb = TB - 1
            for c in range(1, NC + 1):
                for which in order(c):
                    if c < NC:
                        shared_up(tb * NC + c, tb, c, which)
                    else:
                        step_up(0, 0, which, 0)
                shared_down(tb * NC + (c - 1), tb, c - 1)
                if c - 1 in TOKENS_AFTER:
                    turn_tokens(0, TOKENS_AFTER.index(c - 1), 0, 16 * (ST // P))

            def step(k, p, fills):
                for c in range(1, NC + 1):
                    for which in order(c):
                        if c < NC:
                            step_up(k, c, which, p)
                        else:
                            step_up(k + 1, 0, which, 1 - p)
                    step_down(k, c - 1, p)
                    if c - 1 in TOKENS_AFTER:
                        turn_tokens(k + 1, TOKENS_AFTER.index(c - 1), 1 - p, fills)

            step(0, 0, 16 * (ST // P))
            step(1, 1, 2 * 16 * (ST // P))
            with pe.Fori(1, (STEPS - 1) // 2) as half:
                step(2 * half, 0, half * (16 * (ST // P)) + 16 * (ST // P))
                step(2 * half + 1, 1, half * (16 * (ST // P)) + 2 * 16 * (ST // P))
            k = STEPS - 1
            for c in range(1, NC):
                for which in range(2):
                    step_up(k, c, which, 0)
                step_down(k, c - 1, 0)
            step_down(k, NC - 1, 0)


_INS = ["x", "ctx_2048", "L0_xattn_ssm_kernel", "L0_xattn_D", "L0_ffn_sw1", "L0_ffn_sw2", "L0_ffn_sw3",
        "L0_ffn_ew1", "L0_ffn_ew2", "L0_ffn_ew3", "L0_ffn_wr"]


def kernel(**inputs):
    import numpy as _np
    import concourse.bacc as _bacc
    from concourse import mybir as _mybir
    from concourse.bass_utils import run_bass_kernel_spmd as _run

    nc = _bacc.Bacc("TRN2", target_bir_lowering=False, num_devices=1)
    arrays, args = {}, []
    for name in _INS:
        a = _np.ascontiguousarray(inputs[name])
        arrays[f"in_{name}_dram"] = a
        args.append(nc.dram_tensor(f"in_{name}_dram", a.shape, _mybir.dt.from_np(a.dtype), kind="ExternalInput").ap())
    out = nc.dram_tensor("out_0_dram", (BATCH, CH, L), _mybir.dt.float32, kind="ExternalOutput").ap()
    build(nc, *args, out)
    r = _run(nc, [arrays], core_ids=[0])
    return r.results[0]["out_0_dram"]
```
